# Optimizing a Trainium2 kernel written in Bass

```python
import numpy as np
import jax
import jax.numpy as jnp

def _softmax(x, axis=-1):
    return jax.nn.softmax(x, axis=axis)

def _gelu(x):
    return jax.nn.gelu(x, approximate=True)

def _silu(x):
    return jax.nn.silu(x)

def _sigmoid(x):
    return jax.nn.sigmoid(x)

def _layernorm(x, axis=-1, eps=1e-05):
    m = jnp.mean(x, axis=axis, keepdims=True)
    v = jnp.var(x, axis=axis, keepdims=True)
    return (x - m) / jnp.sqrt(v + eps)

def _scatter_add(tgt, idx, src, axis=0):
    return tgt.at[idx].add(src)

def _segment_sum(src, seg, n):
    return jax.ops.segment_sum(src, seg, n)
kernel_name = 'mk_adj_resnorm_d1_adj_r2_491d62'

def setup_inputs(seed: int=0):
    np.random.seed(seed)
    _w = jnp.asarray

    def _rec_inputs():
        import jax
        import jax.numpy as jnp
        _gk = jax.random.key(seed)
        x = -1.394e-06 + 0.9999 * jax.random.normal(jax.random.fold_in(_gk, 1), (8192, 256), jnp.float32)
        _w = (1.0 + jnp.arange(8192, dtype=jnp.float32)) ** (-0.5)
        _w = _w / _w.mean()
        _pij = jnp.clip(0.000244141 * _w[:, None] * _w[None, :], 0.0, 1.0)
        _a = jax.random.uniform(jax.random.fold_in(_gk, 2), (8192, 8192)) < _pij
        adj = _a.astype(jnp.int32)
        return (x, adj)
    x, adj = _rec_inputs()

    def _L0_gnn_setup():
        import jax, jax.numpy as jnp
        import numpy as np
        N = 4096
        IN_F = 256
        OUT_F = 256
        ALPHA = 0.2
        NEG_BIG = -9000000000000000.0
        key = jax.random.key(seed)
        k1, k2, k3, k4 = jax.random.split(key, 4)
        adjacency = jax.random.randint(k1, (N, N), 0, 2, dtype=jnp.int32)
        features = jax.random.normal(k2, (N, IN_F), dtype=jnp.float32)
        W = jax.random.normal(k3, (IN_F, OUT_F), dtype=jnp.float32) * (1.0 / np.sqrt(IN_F))
        attn = jax.random.normal(k4, (2 * OUT_F, 1), dtype=jnp.float32) * 0.05
        return {'adjacency': adjacency, 'features': features, 'W': W, 'attn': attn}
    _L0_gnn_all = _L0_gnn_setup()
    _L0_gnn_in = {k: v for k, v in _L0_gnn_all.items() if k in ('W', 'attn')}
    del _L0_gnn_all
    return {'x': x, 'adj': adj, 'L0_gnn_W': _L0_gnn_in['W'], 'L0_gnn_attn': _L0_gnn_in['attn']}

def reference(x, adj, L0_gnn_W, L0_gnn_attn):
    import jax
    import jax.numpy as jnp

    def _L0_gnn_ref(adjacency, features, W, attn):
        import jax, jax.numpy as jnp
        import numpy as np
        N = 4096
        IN_F = 256
        OUT_F = 256
        ALPHA = 0.2
        NEG_BIG = -9000000000000000.0
        h = features @ W
        a1 = attn[:OUT_F, 0]
        a2 = attn[OUT_F:, 0]
        s1 = h @ a1
        s2 = h @ a2
        e = jax.nn.leaky_relu(s1[:, None] + s2[None, :], negative_slope=ALPHA)
        e = jnp.where(adjacency > 0, e, NEG_BIG)
        attention = jax.nn.softmax(e, axis=1)
        h_prime = attention @ h
        return jax.nn.elu(h_prime)
    x = _layernorm(x + _L0_gnn_ref(adj, x, L0_gnn_W, L0_gnn_attn), axis=-1)
    return x

_drawn_inputs = setup_inputs


def setup_inputs(seed=0):
    import zlib

    import numpy as np

    out = dict(_drawn_inputs(seed))
    spreads = {}
    factors = {}
    for name, (base, spread) in spreads.items():
        noise = np.random.default_rng([zlib.crc32(name.encode()), seed]).standard_normal(out[name].shape)
        drawn = base * np.exp(spread * noise) if base else spread * noise
        out[name] = jnp.asarray(drawn.astype(out[name].dtype))
    for name, factor in factors.items():
        out[name] = (out[name] * factor).astype(out[name].dtype)
    return out
```

```python
from contextlib import ExitStack

import numpy as np

import concourse.bass as bass
from concourse import mybir

F32 = mybir.dt.float32
I32 = mybir.dt.int32
U32 = mybir.dt.uint32
U8 = mybir.dt.uint8
BF16 = mybir.dt.bfloat16
ALU = mybir.AluOpType
ACT = mybir.ActivationFunctionType
AX_X = mybir.AxisListType.X

P = 128
SLOPE = 0.2
NEG_BIG = -9.0e15
EPS = 1e-5
K = 8
RING = 3


def gat_resnorm(nc, x, adj, W, attn, out):
    N, D = x.shape
    T = N // P
    C = D // P
    DA = D + 2
    GROUP = 2
    G = T // GROUP

    x_tiles = x.rearrange("(t p) d -> p t d", p=P)
    adj_tiles = adj.rearrange("(t p) n -> p t n", p=P)
    out_tiles = out.rearrange("(t p) d -> p t d", p=P)
    haug = nc.dram_tensor("haug", (N, DA), F32).ap()
    s2_row = nc.dram_tensor("s2_row", (T, P), F32).ap()
    haug_groups = haug.rearrange("(g u p) d -> p g u d", p=P, u=GROUP)

    with ExitStack() as ctx:
        def sb(name, shape, dt):
            return ctx.enter_context(nc.sbuf_tensor(name, shape, dt))

        def ps(name, shape):
            return ctx.enter_context(nc.psum_tensor(name, shape, F32))

        def sem(name):
            return ctx.enter_context(nc.semaphore(name))

        X = sb("X", [P, T, D], F32)
        ADJ = sb("ADJ", [P, RING, N + K], I32)
        GATH = sb("GATH", [P, RING, K * DA], F32)
        count_junk = sb("count_junk", [P, N], U8)
        ident = sb("ident", [P, P], F32)
        ones = sb("ones", [P, P], F32)
        Waug = sb("Waug", [P, C, DA], F32)
        mean_h = sb("mean_h", [P, D], F32)
        diag = sb("diag", [P, K + 1, P], F32)
        S12 = sb("S12", [P, T, 2], F32)
        heavy = sb("heavy", [P, T], F32)
        found_at = sb("found_at", [P, RING, K], U32)
        one8 = sb("one8", [P, K], F32)
        gate = sb("gate", [P, 2, RING], F32)
        pool_gate = sb("pool_gate", [P, 1], F32)
        zero2 = sb("zero2", [P, GROUP, 2], F32)
        degree = sb("degree", [P, RING], F32)
        valid = sb("valid", [P, RING, K], F32)
        found = sb("found", [P, RING], F32)
        penalty = sb("penalty", [P, RING, K], F32)
        z = sb("z", [P, K], F32)
        lz = sb("lz", [P, K], F32)
        logits = sb("logits", [P, K], F32)
        row_max = sb("row_max", [P, 1], F32)
        neg_max = sb("neg_max", [P, 1], F32)
        expd = sb("expd", [P, K], F32)
        den = sb("den", [P, 1], F32)
        rden = sb("rden", [P, 1], F32)
        weight = sb("weight", [P, K + 1], F32)
        e_elu = sb("e_elu", [P, D], F32)
        stats = sb("stats", [P, 6], F32)
        mean_var = sb("mean_var", [P, RING, 2], F32)
        veps = sb("veps", [P, 1], F32)
        rstd = sb("rstd", [P, 1], F32)
        Y = sb("Y", [P, RING, D], F32)
        eps = sb("eps", [P, 1], F32)
        minus_half = sb("minus_half", [P, 1], F32)

        HB = [GATH[:, b, 0:GROUP * DA].rearrange("p (u d) -> p u d", u=GROUP) for b in range(2)]
        XS = [GATH[:, b, 520:520 + GROUP * D].rearrange("p (u d) -> p u d", u=GROUP) for b in range(2)]
        XT = [GATH[:, 2, b * GROUP * D:(b + 1) * GROUP * D] for b in range(2)]
        prep = ADJ[:, RING - 1, :].bitcast(F32)
        W_T = prep[:, 0:C * C * P].rearrange("p (o k) -> p o k", o=C)
        a12 = prep[:, 512:512 + 2 * C].rearrange("p (a o) -> p o a", o=C)
        h_sum = prep[:, 1024:1024 + GROUP * DA].rearrange("p (u d) -> p u d", u=GROUP)

        rows_adj = ADJ[:, 0, 0:N]
        pen = ADJ[:, 0, 0:N].bitcast(F32)
        s2_all = ADJ[:, 1, 0:N].bitcast(F32)
        probs = ADJ[:, 2, 0:N].bitcast(F32)
        H = X
        rows_h = GATH[:, 0, 0:DA]
        rows_x = GATH[:, 1, 0:D]
        rows_y = GATH[:, 2, 0:D]
        rows_e = GATH[:, 2, D:2 * D]
        rows_sum = GATH[:, 2, 2 * D:3 * D]
        probsT = [diag[:, 4 * b:4 * b + 4, :].rearrange("p a b -> p (a b)") for b in range(2)]
        TH = T // 2
        onehot = count_junk[:].bitcast(BF16).rearrange("p (t q) -> p t q", t=TH)
        before = Waug[:, 1, 0:P]
        iota_q = Waug[:, 1, P:2 * P]
        row_ids = sb("row_ids", [P, T, 3], BF16)
        heavyT = Waug[0:T, 0, 0:P]
        s2T = Waug[0:T, 0, P:2 * P]
        heavy_in_row = sb("heavy_in_row", [P, 1], F32)
        rank = sb("rank", [P, T], F32)
        n_heavy = sb("n_heavy", [P, 1], I32)
        listed = sb("listed", [P, 3], F32)
        list_id = sb("list_id", [P, 2], F32)
        round_rows = sb("round_rows", [P, 1], U32)
        dense_gate = sb("dense_gate", [P, 5], F32)
        chunk_max = sb("chunk_max", [P, 4], F32)
        chunk_den = sb("chunk_den", [P, 4], F32)

        xT_ps = [ps(f"xT_ps{b}", [P, GROUP * D]) for b in range(2)]
        h_ps = [ps(f"h_ps{b}", [P, GROUP, 512]) for b in range(2)]
        acc_ps = [ps(f"acc_ps{b}", [P, D]) for b in range(2)]

        x_loaded = [sem(f"x_loaded{i}") for i in range(4)]
        params_loaded = sem("params_loaded")
        adj_loaded = [sem(f"adj_loaded{r}") for r in range(RING)]
        consts_ready = sem("consts_ready")
        sentinels_ready = sem("sentinels_ready")
        wT_ready = sem("wT_ready")
        wT_copied = sem("wT_copied")
        wa_ready = sem("wa_ready")
        waug_ready = sem("waug_ready")
        x_staged = sem("x_staged")
        xT_ready = sem("xT_ready")
        xT_copied = sem("xT_copied")
        h_ready = sem("h_ready")
        h_copied = sem("h_copied")
        h_used = sem("h_used")
        h_stored = [sem(f"h_stored{b}") for b in range(2)]
        h_summed = sem("h_summed")
        h_mean_ps = sem("h_mean_ps")
        h_mean_ready = sem("h_mean_ready")
        gath_zeroed = sem("gath_zeroed")
        columns_found = sem("columns_found")
        degree_ready = sem("degree_ready")
        masks_ready = sem("masks_ready")
        gathered = [sem(f"gathered{r}") for r in range(RING)]
        softmax_steps = sem("softmax_steps")
        exp_ready = sem("exp_ready")
        weight_steps = sem("weight_steps")
        heavy_noted = sem("heavy_noted")
        diag_ready = sem("diag_ready")
        gate_passed = sem("gate_passed")
        sum_ready = sem("sum_ready")
        elu_exp_ready = sem("elu_exp_ready")
        y_steps = sem("y_steps")
        norm_steps = sem("norm_steps")
        row_normed = sem("row_normed")
        out_stored = [sem(f"out_stored{r}") for r in range(RING)]

        XL = T // 4

        dense_consts = sem("dense_consts")
        h_loaded = sem("h_loaded")
        s2_stored = sem("s2_stored")
        s2_loaded = sem("s2_loaded")
        turned = sem("turned")
        turned_copied = sem("turned_copied")
        ranks_ready = sem("ranks_ready")
        rank_steps = sem("rank_steps")
        rank_ready = sem("rank_ready")
        onehot_ready = sem("onehot_ready")
        onehot_used = sem("onehot_used")
        list_steps = sem("list_steps")
        rows_gathered = sem("rows_gathered")
        adj_gathered = sem("adj_gathered")
        z_ready = sem("z_ready")
        pen_ready = sem("pen_ready")
        masked_ready = sem("masked_ready")
        dense_max = sem("dense_max")
        logits_ready = sem("logits_ready")
        probs_ready = sem("probs_ready")
        probsT_ready = sem("probsT_ready")
        probsT_copied = sem("probsT_copied")
        dense_sum = sem("dense_sum")
        dense_steps = sem("dense_steps")
        dense_exp = sem("dense_exp")
        dense_norm = sem("dense_norm")
        rows_stored = sem("rows_stored")
        round_open = sem("round_open")

        CH = 4
        CW = N // CH
        TB = 4
        NB = T // TB

        def rounds(eng, body):
            eng.wait_ge(rank_steps, 2)
            n = eng.value_load(n_heavy[0:1, 0:1], min_val=0, max_val=N)
            with eng.Fori(0, T) as g:
                with eng.If(n > g * P):
                    body(g)

        block = ctx.enter_context(nc.Block())

        def known(g):
            return isinstance(g, int)

        class Tile:

            def __init__(self, i, c, unroll):
                self.i, self.c, self.unroll = i, c, unroll
                self.t = unroll * i + c
                self.r = c % RING
                self.s = c % 2
                self.loads = unroll // RING * i + c // RING + 1

            def back(self, n):
                return Tile(self.i, self.c - n, self.unroll)

            def after(self, n):
                return not known(self.i) or self.c >= n

        PEEL = 4

        def over_tiles(eng, step, unroll, lag):
            for t in range(PEEL):
                step(Tile(0, t, unroll))
            with eng.Fori(0, (T - PEEL) // unroll) as i:
                for u in range(unroll):
                    step(Tile(i, PEEL + u, unroll))
            for t in range(T, T + lag):
                step(Tile(0, t, unroll))

        @block.sync
        def _(sp):
            sp.dma_start(Waug[:, :, 0:D], W.rearrange("(c p) d -> p c d", p=P)).then_inc(params_loaded, 16)
            sp.dma_start(prep[:, 512:512 + 2 * C], attn.rearrange("(c p) one -> p (c one)", p=P),
                         allow_slow_non_contiguous=True).then_inc(params_loaded, 16)
            for i in range(4):
                sp.dma_start(X[:, i * XL:(i + 1) * XL, :],
                             x_tiles[:, i * XL:(i + 1) * XL, :]).then_inc(x_loaded[i], 16)
                if i < RING - 1:
                    sp.dma_start(ADJ[:, i, 0:N], adj_tiles[:, i, :]).then_inc(adj_loaded[i], 16)
            for b in range(2):
                sp.wait_ge(h_copied, b + 1)
                sp.dma_start(haug_groups[:, b], HB[b]).then_inc(h_stored[b], 16)
            with sp.Fori(1, G // 2) as i:
                for b in range(2):
                    sp.wait_ge(h_copied, 2 * i + b + 1)
                    sp.dma_start(haug_groups[:, 2 * i + b], HB[b]).then_inc(h_stored[b], 16)
            sp.wait_ge(h_mean_ps, 1)
            sp.dma_start(ADJ[:, RING - 1, 0:N], adj_tiles[:, RING - 1, :]).then_inc(adj_loaded[RING - 1], 16)

            def load_next(a):
                sp.wait_ge(columns_found, a.t + 1)
                sp.wait_ge(degree_ready, a.t + 1)
                sp.dma_start(ADJ[:, a.r, 0:N], adj_tiles[:, bass.ds(a.t + RING, 1), :])\
                    .then_inc(adj_loaded[a.r], 16)

            def store(a):
                sp.wait_ge(row_normed, a.t + 1)
                sp.dma_start(out_tiles[:, bass.ds(a.t, 1), :], Y[:, a.r:a.r + 1, :])\
                    .then_inc(out_stored[a.r], 16)

            for t in range(PEEL):
                load_next(Tile(0, t, RING))
                if t >= 3:
                    store(Tile(0, t - 3, RING))
            with sp.Fori(0, (T - PEEL) // RING - 1) as i:
                for u in range(RING):
                    a = Tile(i, PEEL + u, RING)
                    load_next(a)
                    store(a.back(3))
            for t in range(T - RING - 3, T):
                store(Tile(0, t, RING))
            sp.wait_ge(y_steps, 4 * T)
            sp.dma_start(H[:], haug.rearrange("(t p) d -> p t d", p=P)[:, :, 0:D]).then_inc(h_loaded, 16)
            sp.wait_ge(turned_copied, 2)
            sp.dma_start(s2_row, s2T).then_inc(s2_stored, 16)
            sp.wait_ge(s2_stored, 16)
            sp.dma_start(s2_all, s2_row.rearrange("t p -> (t p)").partition_broadcast(P))\
                .then_inc(s2_loaded, 16)
            for r in range(RING):
                sp.wait_ge(out_stored[r], 16 * len(range(r, T, RING)))
            sp.wait_ge(h_loaded, 16)
            sp.wait_ge(s2_loaded, 16)

        @block.tensor
        def _(pe):
            pe.wait_ge(params_loaded, 32)
            pe.wait_ge(consts_ready, 5)
            for o in range(C):
                for k in range(C):
                    done = nc.tensor.transpose(xT_ps[0][:, (o * C + k) * P:(o * C + k + 1) * P],
                                               Waug[:, k, o * P:(o + 1) * P], ident[:])
            done.then_inc(wT_ready, 1)
            pe.wait_ge(wT_copied, 1)
            for k in range(C):
                for o in range(C):
                    done = nc.tensor.matmul(h_ps[0][:, 0, 2 * k:2 * k + 2], W_T[:, o, k * P:(k + 1) * P],
                                            a12[:, o, :], start=(o == 0), stop=(o == C - 1))
            done.then_inc(wa_ready, 1)
            pe.wait_ge(waug_ready, 2)

            def transposes(g, b):
                pe.wait_ge(x_staged, g + 1)
                for u in range(GROUP):
                    for c in range(C):
                        at = (u * C + c) * P
                        done = nc.tensor.transpose(xT_ps[b][:, at:at + P],
                                                   XS[b][:, u, c * P:(c + 1) * P], ident[:])
                done.then_inc(xT_ready, 1)

            def project(g, b):
                pe.wait_ge(xT_copied, g + 1)
                if not known(g) or g >= 2:
                    pe.wait_ge(h_copied, g - 1)
                for u in range(GROUP):
                    for c in range(C):
                        at = (u * C + c) * P
                        done = nc.tensor.matmul(h_ps[b][:, u, 0:DA], XT[b][:, at:at + P], Waug[:, c, :],
                                                start=(c == 0), stop=(c == C - 1))
                done.then_inc(h_ready, 1)

            transposes(0, 0)
            transposes(1, 1)
            for b in range(2):
                project(b, b)
                transposes(b + 2, b)
            with pe.Fori(1, G // 2 - 1) as i:
                for b in range(2):
                    project(2 * i + b, b)
                    transposes(2 * i + b + 2, b)
            project(G - 2, 0)
            project(G - 1, 1)

            pe.wait_ge(h_summed, 1)
            nc.tensor.matmul(acc_ps[0][:], ones[:], h_sum[:, 0, 0:D], start=True, stop=True)\
                .then_inc(h_mean_ps, 1)
            pe.wait_ge(h_mean_ready, 1)

            def step(a):
                pe.wait_ge(diag_ready, a.t + 1)
                if a.after(2):
                    pe.wait_ge(y_steps, 4 * (a.t - 1))
                    pe.wait_ge(elu_exp_ready, a.t - 1)
                for k in range(K + 1):
                    rows = GATH[:, a.r, k * DA:k * DA + D] if k < K else mean_h[:]
                    done = nc.tensor.matmul(acc_ps[a.s][:], diag[:, k, :], rows, start=(k == 0), stop=(k == K))
                done.then_inc(sum_ready, 1)

            over_tiles(pe, step, 2 * RING, 0)

            pe.wait_ge(heavy_noted, T)
            pe.wait_ge(dense_consts, 5)
            nc.tensor.transpose(xT_ps[0][0:T, 0:P], heavy[:], ident[:])
            nc.tensor.transpose(xT_ps[0][0:T, P:2 * P], S12[:, :, 1], ident[:]).then_inc(turned, 1)
            pe.wait_ge(turned_copied, 3)
            nc.tensor.matmul(xT_ps[1][:, 0:T], heavyT, before[0:T, 0:T], start=True, stop=False)
            nc.tensor.matmul(xT_ps[1][:, 0:T], before, heavy_in_row[:].broadcast_to([P, T]),
                             start=False, stop=True)
            nc.tensor.matmul(h_ps[0][:, 0, 0:1], ones[:], heavy_in_row[:], start=True, stop=True)\
                .then_inc(ranks_ready, 1)
            pe.wait_ge(h_loaded, 16)

            def dense_round(g):
                for half in range(2):
                    pe.wait_ge(onehot_ready, 2 * g + half + 1)
                    for t in range(TH):
                        done = nc.tensor.matmul(h_ps[0][:, 0, 0:3], onehot[:, t, :], row_ids[:, half * TH + t, :],
                                                start=(half == 0 and t == 0), stop=(half == 1 and t == TH - 1))
                    done.then_inc(onehot_used, 1)
                for n in range(NB + 1):
                    if n < NB:
                        if n % (NB // CH) == 0:
                            pe.wait_ge(probs_ready, CH * g + n // (NB // CH) + 1)
                        if n >= 2:
                            pe.wait_ge(probsT_copied, NB * g + n - 1)
                        for u in range(TB):
                            at = (n * TB + u) * P
                            done = nc.tensor.transpose(xT_ps[n % 2][:, u * P:(u + 1) * P], probs[:, at:at + P],
                                                       ident[:])
                        done.then_inc(probsT_ready, 1)
                    if n >= 1:
                        m = n - 1
                        pe.wait_ge(probsT_copied, NB * g + m + 1)
                        for u in range(TB):
                            done = nc.tensor.matmul(acc_ps[0][:], probsT[m % 2][:, u * P:(u + 1) * P],
                                                    H[:, m * TB + u, :], start=(m == 0 and u == 0),
                                                    stop=(m == NB - 1 and u == TB - 1))
                        done.then_inc(dense_sum, 1)

            rounds(pe, dense_round)

        @block.vector
        def _(dve):
            dve.memset(one8[:], 1.0).then_inc(sentinels_ready, 1)
            dve.memset(ADJ[:, :, N:N + K], 1).then_inc(sentinels_ready, 1)
            dve.wait_ge(wT_ready, 1)
            dve.tensor_copy(prep[:, 0:C * C * P], xT_ps[0][:, 0:C * C * P]).then_inc(wT_copied, 1)
            dve.wait_ge(wa_ready, 1)
            for k in range(C):
                dve.tensor_copy(Waug[:, k, D:DA], h_ps[0][:, 0, 2 * k:2 * k + 2]).then_inc(waug_ready, 1)

            def copy_xT(g, b):
                dve.wait_ge(xT_ready, g + 1)
                if not known(g) or g >= 2:
                    dve.wait_ge(h_ready, g - 1)
                dve.tensor_copy(XT[b], xT_ps[b][:]).then_inc(xT_copied, 1)

            copy_xT(0, 0)
            copy_xT(1, 1)
            with dve.Fori(1, G // 2) as i:
                for b in range(2):
                    copy_xT(2 * i + b, b)
            dve.wait_ge(h_mean_ps, 1)
            dve.tensor_scalar(mean_h[:], acc_ps[0][:], 1.0 / N, None, ALU.mult).then_inc(h_mean_ready, 1)
            for b in range(2):
                dve.wait_ge(h_stored[b], 16 * (G // 2))
            dve.wait_ge(h_used, G + 1)
            dve.wait_ge(h_ready, G)
            dve.memset(GATH[:], 0.0).then_inc(gath_zeroed, 1)
            dve.wait_ge(sentinels_ready, 2)
            dve.wait_ge(gath_zeroed, 1)

            def masks(a):
                dve.wait_ge(columns_found, a.t + 1)
                dve.tensor_scalar(valid[:, a.r, :], found_at[:, a.r, :], float(N) - 0.5, None, ALU.is_lt)\
                    .then_inc(masks_ready, 1)
                dve.tensor_scalar(penalty[:, a.r, :], found_at[:, a.r, :], float(N) - 0.5, NEG_BIG,
                                  ALU.is_gt, ALU.mult).then_inc(masks_ready, 1)
                dve.wait_ge(masks_ready, 3 * a.t + 2)
                dve.tensor_reduce(found[:, a.r:a.r + 1], valid[:, a.r, :], AX_X, ALU.add)\
                    .then_inc(masks_ready, 1)

            def logits_of(a):
                dve.wait_ge(gathered[a.r], 16 * K * a.loads)
                dve.wait_ge(masks_ready, 3 * a.t + 3)
                if a.after(1):
                    dve.wait_ge(exp_ready, a.t)
                s2 = GATH[:, a.r, :].rearrange("p (k d) -> p k d", k=K)[:, :, D + 1]
                dve.tensor_scalar(z[:], s2, S12[:, bass.ds(a.t, 1), 0], None, ALU.add)\
                    .then_inc(softmax_steps, 1)
                dve.wait_ge(softmax_steps, 4 * a.t + 1)
                dve.scalar_tensor_tensor(out=lz[:], in0=z[:], scalar=SLOPE, in1=z[:], op0=ALU.mult,
                                         op1=ALU.max).then_inc(softmax_steps, 1)
                dve.wait_ge(softmax_steps, 4 * a.t + 2)
                dve.tensor_tensor(logits[:], lz[:], penalty[:, a.r, :], ALU.add).then_inc(softmax_steps, 1)
                dve.wait_ge(softmax_steps, 4 * a.t + 3)
                dve.tensor_reduce(neg_max[:], logits[:], AX_X, ALU.max, negate=True)\
                    .then_inc(softmax_steps, 1)

            def note_heavy(a):
                dve.wait_ge(degree_ready, a.t + 1)
                dve.tensor_tensor(heavy[:, bass.ds(a.t, 1)], degree[:, a.r:a.r + 1], found[:, a.r:a.r + 1],
                                  ALU.not_equal).then_inc(heavy_noted, 1)

            def weights_of(a):
                dve.wait_ge(exp_ready, a.t + 1)
                if a.after(1):
                    dve.wait_ge(diag_ready, a.t)
                dve.reciprocal(rden[:], den[:]).then_inc(weight_steps, 1)
                dve.tensor_scalar(weight[:, K:K + 1], found[:, a.r:a.r + 1], 0.0, None, ALU.is_equal)\
                    .then_inc(weight_steps, 1)
                dve.wait_ge(weight_steps, 3 * a.t + 2)
                dve.scalar_tensor_tensor(out=weight[:, 0:K], in0=expd[:], scalar=rden[:, 0:1],
                                         in1=valid[:, a.r, :], op0=ALU.mult, op1=ALU.mult)\
                    .then_inc(weight_steps, 1)

            def residual(a):
                dve.wait_ge(sum_ready, a.t + 1)
                dve.wait_ge(elu_exp_ready, a.t + 1)
                if a.after(RING):
                    dve.wait_ge(out_stored[a.r], 16 * (a.loads - 1))
                y = Y[:, a.r, :]
                dve.scalar_tensor_tensor(out=Y[:, a.r:a.r + 1, :], in0=acc_ps[a.s][:].rearrange("p (a d) -> p a d", a=1),
                                         scalar=0.0, in1=X[:, bass.ds(a.t, 1), :], op0=ALU.max, op1=ALU.add)\
                    .then_inc(y_steps, 1)
                dve.wait_ge(y_steps, 4 * a.t + 1)
                dve.scalar_tensor_tensor(out=y, in0=e_elu[:], scalar=1.0, in1=y, op0=ALU.min,
                                         op1=ALU.add).then_inc(y_steps, 1)
                dve.wait_ge(y_steps, 4 * a.t + 2)
                dve.bn_stats(stats[:], y).then_inc(y_steps, 1)
                dve.wait_ge(y_steps, 4 * a.t + 3)
                if a.after(RING):
                    dve.wait_ge(row_normed, a.t - RING + 1)
                dve.memset(gate[:, 1, a.r:a.r + 1], 0.0)
                dve.bn_aggr(mean_var[:, a.r, :], stats[:]).then_inc(y_steps, 1)

            def step(a):
                inside = not (known(a.i) and a.c >= T)
                if inside:
                    if a.after(RING):
                        dve.wait_ge(weight_steps, 3 * (a.t - RING + 1))
                    dve.wait_ge(adj_loaded[a.r], 16 * a.loads)
                    dve.memset(gate[:, 0, a.r:a.r + 1], 0.0)
                    dve.max_index(found_at[:, a.r, :], one8[:], ADJ[:, a.r, :]).then_inc(columns_found, 1)
                    masks(a)
                if a.after(1) and not (known(a.i) and a.c > T):
                    logits_of(a.back(1))
                    note_heavy(a.back(1))
                if a.after(2):
                    residual(a.back(2))
                if a.after(1) and not (known(a.i) and a.c > T):
                    weights_of(a.back(1))

            over_tiles(dve, step, 2 * RING, 2)

            dve.wait_ge(turned, 1)
            dve.tensor_copy(heavyT, xT_ps[0][0:T, 0:P]).then_inc(turned_copied, 1)
            dve.tensor_copy(s2T, xT_ps[0][0:T, P:2 * P]).then_inc(turned_copied, 1)
            dve.wait_ge(heavy_noted, T)
            dve.tensor_reduce(heavy_in_row[:], heavy[:], AX_X, ALU.add).then_inc(turned_copied, 1)
            dve.wait_ge(ranks_ready, 1)
            dve.scalar_tensor_tensor(out=rank[:], in0=xT_ps[1][:, 0:T], scalar=1.0, in1=heavy[:], op0=ALU.add,
                                     op1=ALU.mult).then_inc(rank_steps, 1)
            dve.tensor_copy(n_heavy[:], h_ps[0][:, 0, 0:1]).then_inc(rank_steps, 1)
            dve.wait_ge(rank_steps, 1)
            dve.tensor_scalar(rank[:], rank[:], -1.0, None, ALU.add).then_inc(rank_ready, 1)
            dve.wait_ge(dense_consts, 5)

            def dense_round(g):
                dve.wait_ge(rank_ready, g + 1)
                dve.wait_ge(round_open, g + 1)
                for half in range(2):
                    if half == 1:
                        dve.wait_ge(onehot_used, 2 * g + 1)
                    dve.tensor_tensor(onehot, rank[:, half * TH:(half + 1) * TH].unsqueeze(2).broadcast_to([P, TH, P]),
                                      iota_q.unsqueeze(1).broadcast_to([P, TH, P]), ALU.is_equal)\
                        .then_inc(onehot_ready, 1)
                dve.wait_ge(onehot_ready, 2 * g + 2)
                dve.tensor_scalar(rank[:], rank[:], -float(P), None, ALU.add).then_inc(rank_ready, 1)
                dve.wait_ge(onehot_used, 2 * g + 2)
                dve.tensor_copy(listed[:], h_ps[0][:, 0, 0:3]).then_inc(list_steps, 1)
                dve.wait_ge(list_steps, 4 * g + 1)
                dve.scalar_tensor_tensor(out=list_id[:, 0:1], in0=listed[:, 0:1], scalar=float(P),
                                         in1=listed[:, 1:2], op0=ALU.mult, op1=ALU.add).then_inc(list_steps, 1)
                dve.wait_ge(list_steps, 4 * g + 2)
                dve.scalar_tensor_tensor(out=list_id[:, 1:2], in0=listed[:, 2:3], scalar=-float(N),
                                         in1=list_id[:, 0:1], op0=ALU.mult, op1=ALU.add).then_inc(list_steps, 1)
                dve.wait_ge(list_steps, 4 * g + 3)
                dve.tensor_scalar(round_rows[:], list_id[:, 1:2], float(N), None, ALU.add).then_inc(list_steps, 1)
                dve.wait_ge(adj_gathered, 16 * g + 16)
                for c in range(CH):
                    cols = slice(c * CW, (c + 1) * CW)
                    dve.tensor_scalar(pen[:, cols], rows_adj[:, cols], 0.0, NEG_BIG / SLOPE, ALU.is_le, ALU.mult)\
                        .then_inc(pen_ready, 1)
                for c in range(CH):
                    cols = slice(c * CW, (c + 1) * CW)
                    dve.wait_ge(pen_ready, CH * g + c + 1)
                    dve.wait_ge(z_ready, CH * g + c + 1)
                    dve.memset(dense_gate[:, c:c + 1], 0.0)
                    dve.tensor_tensor_reduce(probs[:, cols], probs[:, cols], pen[:, cols], 1.0, -3.0e38, ALU.add,
                                             ALU.max, chunk_max[:, c:c + 1]).then_inc(masked_ready, 1)
                dve.wait_ge(masked_ready, CH * g + CH)
                dve.tensor_reduce(row_max[:], chunk_max[:], AX_X, ALU.max).then_inc(dense_max, 1)
                dve.wait_ge(dense_max, 3 * g + 1)
                dve.scalar_tensor_tensor(out=lz[:, 0:1], in0=row_max[:], scalar=SLOPE, in1=row_max[:],
                                         op0=ALU.mult, op1=ALU.max).then_inc(dense_max, 1)
                dve.wait_ge(dense_max, 3 * g + 2)
                dve.tensor_scalar(neg_max[:], lz[:, 0:1], -1.0, None, ALU.mult).then_inc(dense_max, 1)
                for c in range(CH):
                    cols = slice(c * CW, (c + 1) * CW)
                    dve.scalar_tensor_tensor(out=probs[:, cols], in0=probs[:, cols], scalar=SLOPE,
                                             in1=probs[:, cols], op0=ALU.mult, op1=ALU.max)\
                        .then_inc(logits_ready, 1)
                for n in range(NB):
                    dve.wait_ge(probsT_ready, NB * g + n + 1)
                    if n >= 2:
                        dve.wait_ge(dense_sum, NB * g + n - 1)
                    dve.tensor_copy(probsT[n % 2], xT_ps[n % 2][:]).then_inc(probsT_copied, 1)
                dve.wait_ge(probs_ready, CH * g + CH)
                dve.tensor_reduce(den[:], chunk_den[:], AX_X, ALU.add).then_inc(dense_steps, 1)
                dve.wait_ge(dense_steps, 7 * g + 1)
                dve.reciprocal(rden[:], den[:]).then_inc(dense_steps, 1)
                dve.wait_ge(dense_steps, 7 * g + 2)
                dve.wait_ge(dense_sum, NB * g + NB)
                dve.tensor_scalar(rows_sum, acc_ps[0][:], rden[:, 0:1], None, ALU.mult).then_inc(dense_steps, 1)
                dve.wait_ge(dense_steps, 7 * g + 3)
                dve.scalar_tensor_tensor(out=rows_y, in0=rows_sum, scalar=0.0, in1=rows_x, op0=ALU.max,
                                         op1=ALU.add).then_inc(dense_steps, 1)
                dve.wait_ge(dense_steps, 7 * g + 4)
                dve.wait_ge(dense_exp, g + 1)
                dve.scalar_tensor_tensor(out=rows_y, in0=rows_e, scalar=1.0, in1=rows_y, op0=ALU.min,
                                         op1=ALU.add).then_inc(dense_steps, 1)
                dve.wait_ge(dense_steps, 7 * g + 5)
                dve.bn_stats(stats[:], rows_y).then_inc(dense_steps, 1)
                dve.wait_ge(dense_steps, 7 * g + 6)
                dve.memset(dense_gate[:, CH:CH + 1], 0.0)
                dve.bn_aggr(mean_var[:, 0, :], stats[:]).then_inc(dense_steps, 1)

            rounds(dve, dense_round)

        @block.scalar
        def _(act):
            def copy_h(g, b):
                act.wait_ge(h_ready, g + 1)
                if not known(g) or g >= 2:
                    act.wait_ge(h_used, g)
                act.activation(HB[b], h_ps[b][:, :, 0:DA], ACT.Copy).then_inc(h_copied, 1)

            copy_h(0, 0)
            copy_h(1, 1)
            with act.Fori(1, G // 2) as i:
                for b in range(2):
                    g = 2 * i + b
                    act.wait_ge(h_ready, g + 1)
                    act.wait_ge(h_used, g)
                    act.wait_ge(h_stored[b], 16 * i)
                    act.activation(HB[b], h_ps[b][:, :, 0:DA], ACT.Copy).then_inc(h_copied, 1)

            def count(a):
                act.wait_ge(adj_loaded[a.r], 16 * a.loads)
                if a.after(1):
                    act.wait_ge(degree_ready, a.t)
                if a.after(RING):
                    act.wait_ge(heavy_noted, a.t - RING + 1)
                act.activation(count_junk[:], ADJ[:, a.r, 0:N], ACT.Copy, accum_out=degree[:, a.r:a.r + 1])\
                    .then_inc(degree_ready, 1)

            def exp_for_elu(a):
                act.wait_ge(sum_ready, a.t + 1)
                if a.after(1):
                    act.wait_ge(y_steps, 4 * (a.t - 1) + 2)
                act.activation(e_elu[:], acc_ps[a.s][:], ACT.Exp).then_inc(elu_exp_ready, 1)

            def exp_and_diag(a):
                act.wait_ge(softmax_steps, 4 * a.t + 4)
                if a.after(1):
                    act.wait_ge(weight_steps, 3 * a.t)
                act.activation(expd[:], logits[:], ACT.Exp, bias=neg_max[:], accum_out=den[:])\
                    .then_inc(exp_ready, 1)
                act.wait_ge(weight_steps, 3 * a.t + 3)
                if a.after(1):
                    act.wait_ge(sum_ready, a.t)
                for k in range(K + 1):
                    done = act.activation(diag[:, k, :], ident[:], ACT.Copy, scale=weight[:, k:k + 1])
                done.then_inc(diag_ready, 1)

            def step(a):
                if not (known(a.i) and a.c >= T):
                    count(a)
                if a.after(2):
                    exp_for_elu(a.back(2))
                if a.after(1) and not (known(a.i) and a.c > T):
                    exp_and_diag(a.back(1))

            over_tiles(act, step, 2 * RING, 2)

            act.wait_ge(s2_loaded, 16)

            def dense_round(g):
                act.wait_ge(rows_gathered, 32 * g + 32)
                for c in range(CH):
                    cols = slice(c * CW, (c + 1) * CW)
                    act.activation(probs[:, cols], s2_all[:, cols], ACT.Identity, bias=rows_h[:, D:D + 1])\
                        .then_inc(z_ready, 1)
                act.wait_ge(dense_max, 3 * g + 3)
                for c in range(CH):
                    act.wait_ge(logits_ready, CH * g + c + 1)
                    cols = slice(c * CW, (c + 1) * CW)
                    act.activation(probs[:, cols], probs[:, cols], ACT.Exp, bias=neg_max[:],
                                   accum_out=chunk_den[:, c:c + 1]).then_inc(probs_ready, 1)
                act.wait_ge(dense_steps, 7 * g + 3)
                act.activation(rows_e, rows_sum, ACT.Exp).then_inc(dense_exp, 1)

            rounds(act, dense_round)

        @block.gpsimd
        def _(pool):
            pool.memset(ones[:], 1.0).then_inc(consts_ready, 1)
            pool.memset(minus_half[:], -0.5).then_inc(consts_ready, 1)
            pool.memset(eps[:], EPS).then_inc(consts_ready, 1)
            pool.memset(zero2[:], 0.0).then_inc(consts_ready, 1)
            pool.wait_ge(consts_ready, 4)
            pool.affine_select(out=ident[:], in_=ones[:], pattern=[[-1, P]], compare_op=ALU.is_equal,
                               fill=0.0, base=0, channel_multiplier=1).then_inc(consts_ready, 1)
            pool.memset(h_sum, 0.0).then_inc(h_used, 1)

            def use_h(g, b):
                pool.wait_ge(h_copied, g + 1)
                pool.wait_ge(h_used, g + 1)
                pool.tensor_tensor(S12[:, bass.ds(GROUP * g, GROUP), :], HB[b][:, :, D:DA], zero2[:], ALU.add)
                pool.tensor_tensor(h_sum, h_sum, HB[b], ALU.add).then_inc(h_used, 1)

            def stage_x(g, b):
                if not known(g) or g >= 2:
                    pool.wait_ge(xT_ready, g - 1)
                pool.tensor_copy(XS[b], X[:, bass.ds(GROUP * g, GROUP), :]).then_inc(x_staged, 1)

            for i in range(4):
                pool.wait_ge(x_loaded[i], 16)
            stage_x(0, 0)
            stage_x(1, 1)
            with pool.Fori(1, G // 2) as i:
                for b in range(2):
                    g = 2 * i + b
                    stage_x(g, b)
                    use_h(g - 2, b)
            use_h(G - 2, 0)
            use_h(G - 1, 1)
            pool.wait_ge(h_used, G + 1)
            pool.tensor_tensor(h_sum[:, 0, :], h_sum[:, 0, :], h_sum[:, 1, :], ALU.add).then_inc(h_summed, 1)
            for b in range(2):
                pool.wait_ge(h_stored[b], 16 * (G // 2))
            pool.wait_ge(gath_zeroed, 1)
            pool.affine_select(out=before, in_=ones[:], pattern=[[1, P]], compare_op=ALU.is_gt, fill=0.0,
                               base=0, channel_multiplier=-1).then_inc(dense_consts, 1)
            pool.iota(iota_q, pattern=[[1, P]], base=0, channel_multiplier=0,
                      allow_small_or_imprecise_dtypes=True).then_inc(dense_consts, 1)
            pool.iota(row_ids[:, :, 0], pattern=[[1, T]], base=0, channel_multiplier=0,
                      allow_small_or_imprecise_dtypes=True).then_inc(dense_consts, 1)
            pool.iota(row_ids[:, :, 1], pattern=[[0, T]], base=0, channel_multiplier=1,
                      allow_small_or_imprecise_dtypes=True).then_inc(dense_consts, 1)
            pool.memset(row_ids[:, :, 2], 1.0).then_inc(dense_consts, 1)

            def gather(a):
                pool.wait_ge(columns_found, a.t + 1)
                if a.after(RING):
                    pool.wait_ge(sum_ready, a.t - RING + 1)
                if a.after(1):
                    pool.wait_ge(gate_passed, a.t)
                pool.tensor_tensor(pool_gate[:], minus_half[:], minus_half[:], ALU.add)\
                    .then_inc(gate_passed, 1)
                for k in range(K):
                    pool.indirect_dma_start(
                        out=GATH[:, a.r, k * DA:(k + 1) * DA], out_offset=None, in_=haug,
                        in_offset=bass.IndirectOffsetOnAxis(ap=found_at[:, a.r, k:k + 1], axis=0),
                        bounds_check=N - 1, oob_is_err=False).then_inc(gathered[a.r], 16)

            def normalise(a):
                pool.wait_ge(y_steps, 4 * a.t + 4)
                if a.after(1):
                    pool.wait_ge(row_normed, a.t)
                pool.tensor_tensor(veps[:], mean_var[:, a.r, 1:2], eps[:], ALU.add).then_inc(norm_steps, 1)
                pool.wait_ge(norm_steps, 3 * a.t + 1)
                pool.tensor_tensor(rstd[:], veps[:], minus_half[:], ALU.pow).then_inc(norm_steps, 1)
                pool.tensor_tensor(Y[:, a.r, :], Y[:, a.r, :], mean_var[:, a.r, 0:1].broadcast_to([P, D]),
                                   ALU.subtract).then_inc(norm_steps, 1)
                pool.wait_ge(norm_steps, 3 * a.t + 3)
                pool.tensor_tensor(Y[:, a.r, :], Y[:, a.r, :], rstd[:].broadcast_to([P, D]), ALU.mult)\
                    .then_inc(row_normed, 1)

            def step(a):
                if not (known(a.i) and a.c >= T):
                    gather(a)
                if a.after(3):
                    normalise(a.back(3))

            over_tiles(pool, step, RING, 3)

            for r in range(RING):
                pool.wait_ge(out_stored[r], 16 * len(range(r, T, RING)))

            pool.tensor_tensor(veps[:], minus_half[:], minus_half[:], ALU.add).then_inc(round_open, 1)

            def dense_round(g):
                rows = bass.IndirectOffsetOnAxis(ap=round_rows[:], axis=0)
                pool.wait_ge(list_steps, 4 * g + 4)
                pool.tensor_tensor(pool_gate[:], minus_half[:], minus_half[:], ALU.add).then_inc(gate_passed, 1)
                pool.indirect_dma_start(out=rows_h, out_offset=None, in_=haug, in_offset=rows,
                                        bounds_check=N - 1, oob_is_err=False).then_inc(rows_gathered, 16)
                pool.indirect_dma_start(out=rows_x, out_offset=None, in_=x, in_offset=rows,
                                        bounds_check=N - 1, oob_is_err=False).then_inc(rows_gathered, 16)
                pool.indirect_dma_start(out=rows_adj, out_offset=None, in_=adj, in_offset=rows,
                                        bounds_check=N - 1, oob_is_err=False).then_inc(adj_gathered, 16)
                pool.wait_ge(dense_steps, 7 * g + 7)
                pool.tensor_tensor(veps[:], mean_var[:, 0, 1:2], eps[:], ALU.add).then_inc(dense_norm, 1)
                pool.wait_ge(dense_norm, 4 * g + 1)
                pool.tensor_tensor(rstd[:], veps[:], minus_half[:], ALU.pow).then_inc(dense_norm, 1)
                pool.tensor_tensor(rows_y, rows_y, mean_var[:, 0, 0:1].broadcast_to([P, D]), ALU.subtract)\
                    .then_inc(dense_norm, 1)
                pool.wait_ge(dense_norm, 4 * g + 3)
                pool.tensor_tensor(rows_y, rows_y, rstd[:].broadcast_to([P, D]), ALU.mult).then_inc(dense_norm, 1)
                pool.wait_ge(dense_norm, 4 * g + 4)
                pool.tensor_tensor(pool_gate[:], minus_half[:], minus_half[:], ALU.add)
                pool.indirect_dma_start(out=out, out_offset=rows, in_=rows_y, in_offset=None,
                                        bounds_check=N - 1, oob_is_err=False).then_inc(rows_stored, 16)
                pool.wait_ge(rows_stored, 16 * g + 16)
                pool.tensor_tensor(veps[:], minus_half[:], minus_half[:], ALU.add).then_inc(round_open, 1)

            rounds(pool, dense_round)


_INS = ['x', 'adj', 'L0_gnn_W', 'L0_gnn_attn']


def kernel(**inputs):
    import concourse.bacc as _bacc
    from concourse import mybir as _mybir
    from concourse.bass_utils import run_bass_kernel_spmd as _run

    nc = _bacc.Bacc("TRN2", target_bir_lowering=False, num_devices=1)
    arrays, args = {}, []
    for name in _INS:
        a = np.ascontiguousarray(inputs[name])
        arrays[f"in_{name}_dram"] = a
        args.append(nc.dram_tensor(f"in_{name}_dram", a.shape, _mybir.dt.from_np(a.dtype),
                                   kind="ExternalInput").ap())
    shape = inputs['x'].shape
    args.append(nc.dram_tensor("out_0_dram", shape, _mybir.dt.float32, kind="ExternalOutput").ap())
    gat_resnorm(nc, *args)
    r = _run(nc, [arrays], core_ids=[0])
    return r.results[0]["out_0_dram"]
```

```python
from contextlib import ExitStack

import numpy as np

import concourse.bass as bass
from concourse import mybir

F32 = mybir.dt.float32
I32 = mybir.dt.int32
U32 = mybir.dt.uint32
U8 = mybir.dt.uint8
BF16 = mybir.dt.bfloat16
ALU = mybir.AluOpType
ACT = mybir.ActivationFunctionType
AX_X = mybir.AxisListType.X

P = 128
SLOPE = 0.2
NEG_BIG = -9.0e15
EPS = 1e-5
FOUND = 8
K = 7
RING = 3


def gat_resnorm(nc, x, adj, W, attn, out):
    N, D = x.shape
    T = N // P
    C = D // P
    DA = D + 2
    GROUP = 2
    G = T // GROUP

    x_tiles = x.rearrange("(t p) d -> p t d", p=P)
    adj_tiles = adj.rearrange("(t p) n -> p t n", p=P)
    out_tiles = out.rearrange("(t p) d -> p t d", p=P)
    haug = nc.dram_tensor("haug", (N, DA), F32).ap()
    s2_row = nc.dram_tensor("s2_row", (T, P), F32).ap()
    haug_groups = haug.rearrange("(g u p) d -> p g u d", p=P, u=GROUP)

    with ExitStack() as ctx:
        def sb(name, shape, dt):
            return ctx.enter_context(nc.sbuf_tensor(name, shape, dt))

        def ps(name, shape):
            return ctx.enter_context(nc.psum_tensor(name, shape, F32))

        def sem(name):
            return ctx.enter_context(nc.semaphore(name))

        X = sb("X", [P, T, D], F32)
        ADJ = sb("ADJ", [P, RING, N + FOUND], I32)
        GATH = sb("GATH", [P, RING, K * DA], F32)
        count_junk = sb("count_junk", [P, N], U8)
        ident = sb("ident", [P, P], F32)
        ones = sb("ones", [P, P], F32)
        Waug = sb("Waug", [P, C, DA], F32)
        mean_h = sb("mean_h", [P, D], F32)
        diag = sb("diag", [P, K + 1, P], F32)
        S12 = sb("S12", [P, T, 2], F32)
        heavy = sb("heavy", [P, T], F32)
        found_at = sb("found_at", [P, RING, FOUND], U32)
        one8 = sb("one8", [P, FOUND], F32)
        gate = sb("gate", [P, 2, RING], F32)
        pool_gate = sb("pool_gate", [P, 1], F32)
        pool_gates = sb("pool_gates", [P, 5], F32)
        zero2 = sb("zero2", [P, GROUP, 2], F32)
        degree = sb("degree", [P, RING], F32)
        valid = sb("valid", [P, RING, K], F32)
        found = sb("found", [P, RING], F32)
        penalty = sb("penalty", [P, RING, K], F32)
        z = sb("z", [P, K], F32)
        lz = sb("lz", [P, K], F32)
        logits = sb("logits", [P, K], F32)
        row_max = sb("row_max", [P, 1], F32)
        neg_max = sb("neg_max", [P, 1], F32)
        expd = sb("expd", [P, K], F32)
        den = sb("den", [P, 1], F32)
        rden = sb("rden", [P, 1], F32)
        weight = sb("weight", [P, K + 1], F32)
        e_elu = sb("e_elu", [P, D], F32)
        stats = sb("stats", [P, 6], F32)
        mean_var = sb("mean_var", [P, RING, 2], F32)
        veps = sb("veps", [P, 1], F32)
        rstd = sb("rstd", [P, 1], F32)
        Y = sb("Y", [P, RING, D], F32)
        eps = sb("eps", [P, 1], F32)
        minus_half = sb("minus_half", [P, 1], F32)

        gath_flat = GATH[:].rearrange("p r f -> p (r f)")
        places = iter(range(0, RING * K * DA, 2))

        def in_gath(n):
            at = next(places)
            for _ in range(n // 2 - 1):
                next(places)
            return gath_flat[:, at:at + n]

        HB = [in_gath(GROUP * DA).rearrange("p (u d) -> p u d", u=GROUP) for _ in range(2)]
        XS = [in_gath(GROUP * D).rearrange("p (u d) -> p u d", u=GROUP) for _ in range(2)]
        XT = [in_gath(GROUP * D) for _ in range(2)]
        h_sum = in_gath(GROUP * DA).rearrange("p (u d) -> p u d", u=GROUP)
        W_T_flat = in_gath(C * D)
        W_T = W_T_flat.rearrange("p (o k) -> p o k", o=C)
        a12_flat = in_gath(2 * C)
        a12 = a12_flat.rearrange("p (a o) -> p o a", o=C)

        CH = 4
        CW = N // CH
        rows_adj = ADJ[:, 0, 0:N]
        logit = ADJ[:, 0, 0:N].bitcast(F32)
        s2_all = ADJ[:, 1, 0:N].bitcast(F32)
        probs = ADJ[:, 2, 0:N].bitcast(F32)
        H = X
        rows_h = gath_flat[:, 0:DA]
        rows_x = gath_flat[:, 260:260 + D]
        rows_y = gath_flat[:, 516:516 + D]
        rows_e = gath_flat[:, 772:772 + D]
        rows_sum = gath_flat[:, 1028:1028 + D]
        slope_z = gath_flat[:, 1284:1284 + CW]
        probsT = [diag[:, 4 * b:4 * b + 4, :].rearrange("p a b -> p (a b)") for b in range(2)]
        TH = T // 2
        onehot = count_junk[:].bitcast(BF16).rearrange("p (t q) -> p t q", t=TH)
        before = Waug[:, 1, 0:P]
        iota_q = Waug[:, 1, P:2 * P]
        row_ids = sb("row_ids", [P, T, 3], BF16)
        heavyT = Waug[0:T, 0, 0:P]
        s2T = Waug[0:T, 0, P:2 * P]
        heavy_in_row = sb("heavy_in_row", [P, 1], F32)
        rank = sb("rank", [P, T], F32)
        n_heavy = sb("n_heavy", [P, 1], I32)
        listed = sb("listed", [P, 3], F32)
        list_id = sb("list_id", [P, 2], F32)
        next_rows = sb("next_rows", [P, 1], U32)
        next_parts = sb("next_parts", [P, CH], U32)
        round_rows = sb("round_rows", [P, 1], U32)
        dense_gate = sb("dense_gate", [P, 6], F32)
        chunk_max = sb("chunk_max", [P, 4], F32)
        chunk_den = sb("chunk_den", [P, 4], F32)

        xT_ps = [ps(f"xT_ps{b}", [P, GROUP * D]) for b in range(2)]
        h_ps = [ps(f"h_ps{b}", [P, GROUP, 512]) for b in range(2)]
        acc_ps = [ps(f"acc_ps{b}", [P, D]) for b in range(2)]

        x_loaded = [sem(f"x_loaded{i}") for i in range(4)]
        params_loaded = sem("params_loaded")
        adj_loaded = [sem(f"adj_loaded{r}") for r in range(RING)]
        consts_ready = sem("consts_ready")
        sentinels_ready = sem("sentinels_ready")
        wT_ready = sem("wT_ready")
        wT_copied = sem("wT_copied")
        wa_ready = sem("wa_ready")
        waug_ready = sem("waug_ready")
        x_staged = sem("x_staged")
        xT_ready = sem("xT_ready")
        xT_copied = sem("xT_copied")
        h_ready = sem("h_ready")
        h_copied = sem("h_copied")
        h_used = sem("h_used")
        h_stored = [sem(f"h_stored{b}") for b in range(2)]
        h_summed = sem("h_summed")
        h_mean_ps = sem("h_mean_ps")
        h_mean_ready = sem("h_mean_ready")
        gath_zeroed = sem("gath_zeroed")
        columns_found = sem("columns_found")
        degree_ready = sem("degree_ready")
        masks_ready = sem("masks_ready")
        gathered = [sem(f"gathered{r}") for r in range(RING)]
        softmax_steps = sem("softmax_steps")
        exp_ready = sem("exp_ready")
        weight_steps = sem("weight_steps")
        heavy_noted = sem("heavy_noted")
        diag_ready = sem("diag_ready")
        gate_passed = sem("gate_passed")
        sum_ready = sem("sum_ready")
        elu_exp_ready = sem("elu_exp_ready")
        y_steps = sem("y_steps")
        norm_steps = sem("norm_steps")
        row_normed = sem("row_normed")
        out_stored = [sem(f"out_stored{r}") for r in range(RING)]

        XL = T // 4

        dense_consts = sem("dense_consts")
        h_loaded = sem("h_loaded")
        s2_stored = sem("s2_stored")
        s2_loaded = sem("s2_loaded")
        s2_turned = sem("s2_turned")
        s2_copied = sem("s2_copied")
        turned = sem("turned")
        turned_copied = sem("turned_copied")
        ranks_ready = sem("ranks_ready")
        rank_steps = sem("rank_steps")
        rank_ready = sem("rank_ready")
        onehot_ready = sem("onehot_ready")
        onehot_used = sem("onehot_used")
        list_steps = sem("list_steps")
        rows_gathered = sem("rows_gathered")
        x_gathered = sem("x_gathered")
        adj_gathered = [sem(f"adj_gathered{c}") for c in range(4)]
        round_taken = sem("round_taken")
        slope_ready = sem("slope_ready")
        pen_ready = sem("pen_ready")
        masked_ready = sem("masked_ready")
        dense_max = sem("dense_max")
        logits_ready = sem("logits_ready")
        probs_ready = sem("probs_ready")
        probsT_ready = sem("probsT_ready")
        probsT_copied = sem("probsT_copied")
        dense_sum = sem("dense_sum")
        dense_steps = sem("dense_steps")
        sum_taken = sem("sum_taken")
        dense_exp = sem("dense_exp")
        dense_norm = sem("dense_norm")
        rows_stored = sem("rows_stored")
        round_open = sem("round_open")

        TB = 4
        NB = T // TB

        def rounds(eng, first, body):
            eng.wait_ge(rank_steps, 2)
            n = eng.value_load(n_heavy[0:1, 0:1], min_val=0, max_val=N)
            EIGHT = 8
            with eng.If(n > 0):
                first()
                with eng.Fori(0, T // EIGHT) as e:
                    with eng.If(n > e * (EIGHT * P)):
                        with eng.Fori(0, EIGHT) as i:
                            g = e * EIGHT + i
                            with eng.If(n > g * P):
                                body(g, lambda: eng.If(n > g * P + P))

        block = ctx.enter_context(nc.Block())

        def known(g):
            return isinstance(g, int)

        class Tile:

            def __init__(self, i, c, unroll):
                self.i, self.c, self.unroll = i, c, unroll
                self.t = unroll * i + c
                self.r = c % RING
                self.s = c % 2
                self.loads = unroll // RING * i + c // RING + 1

            def back(self, n):
                return Tile(self.i, self.c - n, self.unroll)

            def after(self, n):
                return not known(self.i) or self.c >= n

        PEEL = 4

        def over_tiles(eng, step, unroll, lag):
            for t in range(PEEL):
                step(Tile(0, t, unroll))
            with eng.Fori(0, (T - PEEL) // unroll) as i:
                for u in range(unroll):
                    step(Tile(i, PEEL + u, unroll))
            for t in range(T, T + lag):
                step(Tile(0, t, unroll))

        @block.sync
        def _(sp):
            sp.dma_start(Waug[:, :, 0:D], W.rearrange("(c p) d -> p c d", p=P)).then_inc(params_loaded, 16)
            sp.dma_start(a12_flat, attn.rearrange("(c p) one -> p (c one)", p=P),
                         allow_slow_non_contiguous=True).then_inc(params_loaded, 16)
            for i in range(4):
                sp.dma_start(X[:, i * XL:(i + 1) * XL, :],
                             x_tiles[:, i * XL:(i + 1) * XL, :]).then_inc(x_loaded[i], 16)
            for r in range(RING + 1):
                with sp.Fori(0, CH) as c:
                    for b in range(2):
                        g = 2 * c + (2 * CH * r + b)
                        sp.wait_ge(h_copied, g + 1)
                        sp.dma_start(haug_groups[:, bass.ds(g, 1)], HB[b].unsqueeze(1)).then_inc(h_stored[b], 16)
                    if r < RING:
                        sp.dma_start(ADJ[:, r, bass.ds(c * CW, CW)], adj_tiles[:, r, bass.ds(c * CW, CW)])\
                            .then_inc(adj_loaded[r], 16)
            sp.wait_ge(s2_copied, 1)
            sp.dma_start(s2_row, s2T).then_inc(s2_stored, 16)

            def load_next(a):
                sp.wait_ge(columns_found, a.t + 1)
                sp.wait_ge(degree_ready, a.t + 1)
                sp.dma_start(ADJ[:, a.r, 0:N], adj_tiles[:, bass.ds(a.t + RING, 1), :])\
                    .then_inc(adj_loaded[a.r], 16)

            def store(a):
                sp.wait_ge(row_normed, a.t + 1)
                sp.dma_start(out_tiles[:, bass.ds(a.t, 1), :], Y[:, a.r:a.r + 1, :])\
                    .then_inc(out_stored[a.r], 16)

            for t in range(PEEL):
                load_next(Tile(0, t, RING))
                if t >= 3:
                    store(Tile(0, t - 3, RING))
            with sp.Fori(0, (T - PEEL) // RING - 1) as i:
                for u in range(RING):
                    a = Tile(i, PEEL + u, RING)
                    load_next(a)
                    store(a.back(3))
            HL = 8
            h_tiles = haug.rearrange("(t p) d -> p t d", p=P)[:, :, 0:D]

            def load_h(n):
                if n == T // HL - 1:
                    sp.wait_ge(y_steps, 4 * T)
                sp.dma_start(H[:, n * HL:(n + 1) * HL, :], h_tiles[:, n * HL:(n + 1) * HL, :]).then_inc(h_loaded, 16)

            sp.wait_ge(y_steps, 4 * (T - HL))
            for n in range(2):
                load_h(n)
            for n, t in enumerate(range(T - RING - 3, T)):
                if t == T - 3:
                    sp.wait_ge(columns_found, T - 1)
                    sp.wait_ge(degree_ready, T - 1)
                    sp.wait_ge(s2_stored, 16)
                    sp.dma_start(s2_all, s2_row.rearrange("t p -> (t p)").partition_broadcast(P))\
                        .then_inc(s2_loaded, 16)
                store(Tile(0, t, RING))
                load_h(n + 2)
            for r in range(RING):
                sp.wait_ge(out_stored[r], 16 * len(range(r, T, RING)))
            sp.wait_ge(h_loaded, 16 * (T // HL))
            sp.wait_ge(s2_loaded, 16)

        @block.tensor
        def _(pe):
            pe.wait_ge(params_loaded, 32)
            pe.wait_ge(consts_ready, 5)
            for o in range(C):
                for k in range(C):
                    done = nc.tensor.transpose(xT_ps[0][:, (o * C + k) * P:(o * C + k + 1) * P],
                                               Waug[:, k, o * P:(o + 1) * P], ident[:])
            done.then_inc(wT_ready, 1)
            pe.wait_ge(wT_copied, 1)
            for k in range(C):
                for o in range(C):
                    done = nc.tensor.matmul(h_ps[0][:, 0, 2 * k:2 * k + 2], W_T[:, o, k * P:(k + 1) * P],
                                            a12[:, o, :], start=(o == 0), stop=(o == C - 1))
            done.then_inc(wa_ready, 1)
            pe.wait_ge(waug_ready, 2)

            def transposes(g, b):
                pe.wait_ge(x_staged, g + 1)
                for u in range(GROUP):
                    for c in range(C):
                        at = (u * C + c) * P
                        done = nc.tensor.transpose(xT_ps[b][:, at:at + P],
                                                   XS[b][:, u, c * P:(c + 1) * P], ident[:])
                done.then_inc(xT_ready, 1)

            def project(g, b):
                pe.wait_ge(xT_copied, g + 1)
                if not known(g) or g >= 2:
                    pe.wait_ge(h_copied, g - 1)
                for u in range(GROUP):
                    for c in range(C):
                        at = (u * C + c) * P
                        done = nc.tensor.matmul(h_ps[b][:, u, 0:DA], XT[b][:, at:at + P], Waug[:, c, :],
                                                start=(c == 0), stop=(c == C - 1))
                done.then_inc(h_ready, 1)

            transposes(0, 0)
            transposes(1, 1)
            for b in range(2):
                project(b, b)
                transposes(b + 2, b)
            with pe.Fori(1, G // 2 - 1) as i:
                for b in range(2):
                    project(2 * i + b, b)
                    transposes(2 * i + b + 2, b)
            project(G - 2, 0)
            project(G - 1, 1)

            pe.wait_ge(h_summed, 1)
            nc.tensor.transpose(xT_ps[0][0:T, 0:P], S12[:, :, 1], ident[:]).then_inc(s2_turned, 1)
            nc.tensor.matmul(acc_ps[0][:], ones[:], h_sum[:, 0, 0:D], start=True, stop=True)\
                .then_inc(h_mean_ps, 1)
            pe.wait_ge(h_mean_ready, 1)

            def step(a):
                pe.wait_ge(diag_ready, a.t + 1)
                if a.after(2):
                    pe.wait_ge(y_steps, 4 * (a.t - 1))
                    pe.wait_ge(elu_exp_ready, a.t - 1)
                for k in range(K + 1):
                    rows = GATH[:, a.r, k * DA:k * DA + D] if k < K else mean_h[:]
                    done = nc.tensor.matmul(acc_ps[a.s][:], diag[:, k, :], rows, start=(k == 0), stop=(k == K))
                done.then_inc(sum_ready, 1)

            over_tiles(pe, step, 2 * RING, 0)

            pe.wait_ge(heavy_noted, T)
            pe.wait_ge(dense_consts, 5)
            nc.tensor.transpose(xT_ps[0][0:T, 0:P], heavy[:], ident[:]).then_inc(turned, 1)
            pe.wait_ge(turned_copied, 2)
            nc.tensor.matmul(xT_ps[1][:, 0:T], heavyT, before[0:T, 0:T], start=True, stop=False)
            nc.tensor.matmul(xT_ps[1][:, 0:T], before, heavy_in_row[:].broadcast_to([P, T]),
                             start=False, stop=True)
            nc.tensor.matmul(h_ps[0][:, 0, 0:1], ones[:], heavy_in_row[:], start=True, stop=True)\
                .then_inc(ranks_ready, 1)

            def list_rows(g, half):
                pe.wait_ge(onehot_ready, 2 * g + half + 1)
                for t in range(TH):
                    done = nc.tensor.matmul(h_ps[0][:, 0, 0:3], onehot[:, t, :], row_ids[:, half * TH + t, :],
                                            start=(half == 0 and t == 0), stop=(half == 1 and t == TH - 1))
                done.then_inc(onehot_used, 1)

            def first():
                list_rows(0, 0)
                list_rows(0, 1)
                pe.wait_ge(h_loaded, 16 * (T // 8))

            def dense_round(g, more):
                for n in range(NB + 1):
                    if n in (1, 3):
                        with more():
                            list_rows(g + 1, n // 2)
                    if n < NB:
                        if n % (NB // CH) == 0:
                            pe.wait_ge(probs_ready, CH * g + n // (NB // CH) + 1)
                        if n >= 2:
                            pe.wait_ge(probsT_copied, NB * g + n - 1)
                        for u in range(TB):
                            at = (n * TB + u) * P
                            done = nc.tensor.transpose(xT_ps[n % 2][:, u * P:(u + 1) * P], probs[:, at:at + P],
                                                       ident[:])
                        done.then_inc(probsT_ready, 1)
                    if n >= 1:
                        m = n - 1
                        pe.wait_ge(probsT_copied, NB * g + m + 1)
                        if m == 0:
                            pe.wait_ge(sum_taken, g + 1)
                        for u in range(TB):
                            done = nc.tensor.matmul(acc_ps[0][:], probsT[m % 2][:, u * P:(u + 1) * P],
                                                    H[:, m * TB + u, :], start=(m == 0 and u == 0),
                                                    stop=(m == NB - 1 and u == TB - 1))
                        done.then_inc(dense_sum, 1)

            rounds(pe, first, dense_round)

        @block.vector
        def _(dve):
            dve.memset(one8[:], 1.0).then_inc(sentinels_ready, 1)
            dve.memset(ADJ[:, :, N:N + FOUND], 1).then_inc(sentinels_ready, 1)
            dve.wait_ge(wT_ready, 1)
            dve.tensor_copy(W_T_flat, xT_ps[0][:, 0:C * C * P]).then_inc(wT_copied, 1)
            dve.wait_ge(wa_ready, 1)
            for k in range(C):
                dve.tensor_copy(Waug[:, k, D:DA], h_ps[0][:, 0, 2 * k:2 * k + 2]).then_inc(waug_ready, 1)

            def stage_x(g, b):
                dve.tensor_copy(XS[b], X[:, bass.ds(GROUP * g, GROUP), :]).then_inc(x_staged, 1)

            def copy_xT(g, b):
                dve.wait_ge(xT_ready, g + 1)
                if not known(g) or g >= 2:
                    dve.wait_ge(h_ready, g - 1)
                dve.tensor_copy(XT[b], xT_ps[b][:]).then_inc(xT_copied, 1)

            GL = XL // GROUP
            dve.wait_ge(x_loaded[0], 16)
            stage_x(0, 0)
            stage_x(1, 1)
            for g in range(2):
                copy_xT(g, g)
                stage_x(g + 2, g)
            for i in range(4):
                dve.wait_ge(x_loaded[i], 16)
                with dve.Fori(max(GL // 2 * i - 1, 1), GL // 2 * (i + 1) - 1) as j:
                    for b in range(2):
                        copy_xT(2 * j + b, b)
                        stage_x(2 * j + b + 2, b)
            copy_xT(G - 2, 0)
            copy_xT(G - 1, 1)
            dve.wait_ge(s2_turned, 1)
            dve.tensor_copy(s2T, xT_ps[0][0:T, 0:P]).then_inc(s2_copied, 1)
            dve.wait_ge(h_mean_ps, 1)
            dve.tensor_scalar(mean_h[:], acc_ps[0][:], 1.0 / N, None, ALU.mult).then_inc(h_mean_ready, 1)
            dve.wait_ge(sentinels_ready, 2)

            def masks(a):
                dve.wait_ge(columns_found, a.t + 1)
                dve.tensor_scalar(valid[:, a.r, :], found_at[:, a.r, 0:K], float(N) - 0.5, None, ALU.is_lt)\
                    .then_inc(masks_ready, 1)
                dve.tensor_scalar(penalty[:, a.r, :], found_at[:, a.r, 0:K], float(N) - 0.5, NEG_BIG,
                                  ALU.is_gt, ALU.mult).then_inc(masks_ready, 1)
                dve.wait_ge(masks_ready, 3 * a.t + 2)
                dve.tensor_reduce(found[:, a.r:a.r + 1], valid[:, a.r, :], AX_X, ALU.add)\
                    .then_inc(masks_ready, 1)

            def logits_and_residual(a, b):
                if a:
                    dve.wait_ge(gathered[a.r], 16 * K * a.loads)
                    dve.wait_ge(masks_ready, 3 * a.t + 3)
                    if a.after(1):
                        dve.wait_ge(exp_ready, a.t)
                    s2 = GATH[:, a.r, :].rearrange("p (k d) -> p k d", k=K)[:, :, D + 1]
                    dve.tensor_scalar(z[:], s2, S12[:, bass.ds(a.t, 1), 0], None, ALU.add)\
                        .then_inc(softmax_steps, 1)
                if b:
                    y = Y[:, b.r, :]
                    dve.wait_ge(sum_ready, b.t + 1)
                    dve.wait_ge(elu_exp_ready, b.t + 1)
                    if b.after(RING):
                        dve.wait_ge(out_stored[b.r], 16 * (b.loads - 1))
                    dve.scalar_tensor_tensor(out=Y[:, b.r:b.r + 1, :], in0=acc_ps[b.s][:].unsqueeze(1),
                                             scalar=0.0, in1=X[:, bass.ds(b.t, 1), :], op0=ALU.max,
                                             op1=ALU.add).then_inc(y_steps, 1)
                if a:
                    dve.wait_ge(softmax_steps, 4 * a.t + 1)
                    dve.scalar_tensor_tensor(out=lz[:], in0=z[:], scalar=SLOPE, in1=z[:], op0=ALU.mult,
                                             op1=ALU.max).then_inc(softmax_steps, 1)
                if b:
                    dve.wait_ge(y_steps, 4 * b.t + 1)
                    dve.scalar_tensor_tensor(out=y, in0=e_elu[:], scalar=1.0, in1=y, op0=ALU.min,
                                             op1=ALU.add).then_inc(y_steps, 1)
                if a:
                    dve.wait_ge(softmax_steps, 4 * a.t + 2)
                    dve.tensor_tensor(logits[:], lz[:], penalty[:, a.r, :], ALU.add).then_inc(softmax_steps, 1)
                if b:
                    dve.wait_ge(y_steps, 4 * b.t + 2)
                    dve.bn_stats(stats[:], y).then_inc(y_steps, 1)
                if a:
                    dve.wait_ge(softmax_steps, 4 * a.t + 3)
                    dve.tensor_reduce(neg_max[:], logits[:], AX_X, ALU.max, negate=True)\
                        .then_inc(softmax_steps, 1)
                    dve.wait_ge(degree_ready, a.t + 1)
                    dve.tensor_tensor(heavy[:, bass.ds(a.t, 1)], degree[:, a.r:a.r + 1], found[:, a.r:a.r + 1],
                                      ALU.not_equal).then_inc(heavy_noted, 1)
                if b:
                    dve.wait_ge(y_steps, 4 * b.t + 3)
                    if b.after(RING):
                        dve.wait_ge(row_normed, b.t - RING + 1)
                    dve.memset(gate[:, 1, b.r:b.r + 1], 0.0)
                    dve.bn_aggr(mean_var[:, b.r, :], stats[:]).then_inc(y_steps, 1)

            def weights_of(a):
                dve.wait_ge(exp_ready, a.t + 1)
                if a.after(1):
                    dve.wait_ge(diag_ready, a.t)
                dve.reciprocal(rden[:], den[:]).then_inc(weight_steps, 1)
                dve.tensor_scalar(weight[:, K:K + 1], found[:, a.r:a.r + 1], 0.0, None, ALU.is_equal)\
                    .then_inc(weight_steps, 1)
                dve.wait_ge(weight_steps, 3 * a.t + 2)
                dve.scalar_tensor_tensor(out=weight[:, 0:K], in0=expd[:], scalar=rden[:, 0:1],
                                         in1=valid[:, a.r, :], op0=ALU.mult, op1=ALU.mult)\
                    .then_inc(weight_steps, 1)

            def step(a):
                inside = not (known(a.i) and a.c >= T)
                if inside:
                    if a.after(RING):
                        dve.wait_ge(weight_steps, 3 * (a.t - RING + 1))
                    dve.wait_ge(adj_loaded[a.r], 16 * (a.loads + CH - 1))
                    dve.memset(gate[:, 0, a.r:a.r + 1], 0.0)
                    dve.max_index(found_at[:, a.r, :], one8[:], ADJ[:, a.r, :]).then_inc(columns_found, 1)
                    masks(a)
                running = a.after(1) and not (known(a.i) and a.c > T)
                logits_and_residual(a.back(1) if running else None, a.back(2) if a.after(2) else None)
                if running:
                    weights_of(a.back(1))

            over_tiles(dve, step, 2 * RING, 2)

            dve.wait_ge(turned, 1)
            dve.tensor_copy(heavyT, xT_ps[0][0:T, 0:P]).then_inc(turned_copied, 1)
            dve.wait_ge(heavy_noted, T)
            dve.tensor_reduce(heavy_in_row[:], heavy[:], AX_X, ALU.add).then_inc(turned_copied, 1)
            dve.wait_ge(ranks_ready, 1)
            dve.scalar_tensor_tensor(out=rank[:], in0=xT_ps[1][:, 0:T], scalar=1.0, in1=heavy[:], op0=ALU.add,
                                     op1=ALU.mult).then_inc(rank_steps, 1)
            dve.tensor_copy(n_heavy[:], h_ps[0][:, 0, 0:1]).then_inc(rank_steps, 1)
            dve.wait_ge(rank_steps, 1)
            dve.tensor_scalar(rank[:], rank[:], -1.0, None, ALU.add).then_inc(rank_ready, 1)
            dve.wait_ge(dense_consts, 5)
            dve.wait_ge(s2_loaded, 16)
            dve.memset(dense_gate[:], 0.0).then_inc(sum_taken, 1)
            L = 4 + CH

            def prepare(g):
                dve.wait_ge(rank_ready, g + 1)
                if not known(g) or g >= 1:
                    dve.wait_ge(round_taken, g)
                for half in range(2):
                    if half == 1:
                        dve.wait_ge(onehot_used, 2 * g + 1)
                    dve.tensor_tensor(onehot, rank[:, half * TH:(half + 1) * TH].unsqueeze(2).broadcast_to([P, TH, P]),
                                      iota_q.unsqueeze(1).broadcast_to([P, TH, P]), ALU.is_equal)\
                        .then_inc(onehot_ready, 1)
                dve.wait_ge(onehot_ready, 2 * g + 2)
                dve.tensor_scalar(rank[:], rank[:], -float(P), None, ALU.add).then_inc(rank_ready, 1)
                dve.wait_ge(onehot_used, 2 * g + 2)
                dve.tensor_copy(listed[:], h_ps[0][:, 0, 0:3]).then_inc(list_steps, 1)
                dve.wait_ge(list_steps, L * g + 1)
                dve.scalar_tensor_tensor(out=list_id[:, 0:1], in0=listed[:, 0:1], scalar=float(P),
                                         in1=listed[:, 1:2], op0=ALU.mult, op1=ALU.add).then_inc(list_steps, 1)
                dve.wait_ge(list_steps, L * g + 2)
                dve.scalar_tensor_tensor(out=list_id[:, 1:2], in0=listed[:, 2:3], scalar=-float(N),
                                         in1=list_id[:, 0:1], op0=ALU.mult, op1=ALU.add).then_inc(list_steps, 1)
                dve.wait_ge(list_steps, L * g + 3)
                dve.tensor_scalar(next_rows[:], list_id[:, 1:2], float(N), None, ALU.add).then_inc(list_steps, 1)
                for c in range(CH):
                    dve.tensor_scalar(next_parts[:, c:c + 1], list_id[:, 1:2], float(CH), float(CH * N + c),
                                      ALU.mult, ALU.add).then_inc(list_steps, 1)
                for c in range(CH):
                    cols = slice(c * CW, (c + 1) * CW)
                    dve.wait_ge(adj_gathered[c], 16 * g + 16)
                    dve.tensor_scalar(logit[:, cols], rows_adj[:, cols], 0.0, NEG_BIG / SLOPE, ALU.is_le, ALU.mult)\
                        .then_inc(pen_ready, 1)
                    dve.wait_ge(pen_ready, CH * g + c + 1)
                    dve.memset(dense_gate[:, c:c + 1], 0.0)
                    dve.tensor_tensor_reduce(logit[:, cols], logit[:, cols], s2_all[:, cols], 1.0, -3.0e38,
                                             ALU.add, ALU.max, chunk_max[:, c:c + 1]).then_inc(masked_ready, 1)
                dve.wait_ge(masked_ready, CH * g + CH)
                dve.wait_ge(rows_gathered, 16 * g + 16)
                dve.tensor_reduce(row_max[:], chunk_max[:], AX_X, ALU.max).then_inc(dense_max, 1)
                dve.wait_ge(dense_max, 4 * g + 1)
                dve.tensor_tensor(z[:, 0:1], row_max[:], rows_h[:, D:D + 1], ALU.add).then_inc(dense_max, 1)
                dve.wait_ge(dense_max, 4 * g + 2)
                dve.scalar_tensor_tensor(out=lz[:, 0:1], in0=z[:, 0:1], scalar=SLOPE, in1=z[:, 0:1],
                                         op0=ALU.mult, op1=ALU.max).then_inc(dense_max, 1)
                dve.wait_ge(dense_max, 4 * g + 3)
                dve.tensor_scalar(neg_max[:], lz[:, 0:1], -1.0, None, ALU.mult).then_inc(dense_max, 1)
                for c in range(CH):
                    cols = slice(c * CW, (c + 1) * CW)
                    if c >= 1:
                        dve.wait_ge(logits_ready, CH * g + c)
                    dve.tensor_scalar(slope_z, logit[:, cols], rows_h[:, D:D + 1], SLOPE, ALU.add, ALU.mult)\
                        .then_inc(slope_ready, 1)
                    dve.wait_ge(slope_ready, CH * g + c + 1)
                    dve.scalar_tensor_tensor(out=logit[:, cols], in0=logit[:, cols], scalar=rows_h[:, D:D + 1],
                                             in1=slope_z, op0=ALU.add, op1=ALU.max).then_inc(logits_ready, 1)

            def dense_round(g, more):
                with more():
                    prepare(g + 1)
                dve.wait_ge(probs_ready, CH * g + CH)
                dve.tensor_reduce(den[:], chunk_den[:], AX_X, ALU.add).then_inc(dense_steps, 1)
                dve.wait_ge(dense_steps, 7 * g + 1)
                dve.reciprocal(rden[:], den[:]).then_inc(dense_steps, 1)
                dve.wait_ge(dense_steps, 7 * g + 2)
                dve.wait_ge(dense_sum, NB * g + NB)
                dve.wait_ge(round_open, g + 1)
                dve.tensor_scalar(rows_sum, acc_ps[0][:], rden[:, 0:1], None, ALU.mult).then_inc(dense_steps, 1)
                dve.wait_ge(dense_steps, 7 * g + 3)
                dve.memset(dense_gate[:, CH + 1:CH + 2], 0.0).then_inc(sum_taken, 1)
                dve.wait_ge(x_gathered, 16 * g + 16)
                dve.scalar_tensor_tensor(out=rows_y, in0=rows_sum, scalar=0.0, in1=rows_x, op0=ALU.max,
                                         op1=ALU.add).then_inc(dense_steps, 1)
                dve.wait_ge(dense_steps, 7 * g + 4)
                dve.wait_ge(dense_exp, g + 1)
                dve.scalar_tensor_tensor(out=rows_y, in0=rows_e, scalar=1.0, in1=rows_y, op0=ALU.min,
                                         op1=ALU.add).then_inc(dense_steps, 1)
                dve.wait_ge(dense_steps, 7 * g + 5)
                dve.bn_stats(stats[:], rows_y).then_inc(dense_steps, 1)
                dve.wait_ge(dense_steps, 7 * g + 6)
                dve.memset(dense_gate[:, CH:CH + 1], 0.0)
                dve.bn_aggr(mean_var[:, 0, :], stats[:]).then_inc(dense_steps, 1)

            rounds(dve, lambda: prepare(0), dense_round)

        @block.scalar
        def _(act):
            def copy_h(g, b):
                act.wait_ge(h_ready, g + 1)
                if not known(g) or g >= 2:
                    act.wait_ge(h_used, g)
                act.activation(HB[b], h_ps[b][:, :, 0:DA], ACT.Copy).then_inc(h_copied, 1)

            copy_h(0, 0)
            copy_h(1, 1)
            with act.Fori(1, G // 2) as i:
                for b in range(2):
                    g = 2 * i + b
                    act.wait_ge(h_ready, g + 1)
                    act.wait_ge(h_used, g)
                    act.wait_ge(h_stored[b], 16 * i)
                    act.activation(HB[b], h_ps[b][:, :, 0:DA], ACT.Copy).then_inc(h_copied, 1)

            def count(a):
                act.wait_ge(adj_loaded[a.r], 16 * (a.loads + CH - 1))
                if a.after(1):
                    act.wait_ge(degree_ready, a.t)
                if a.after(RING):
                    act.wait_ge(heavy_noted, a.t - RING + 1)
                act.activation(count_junk[:], ADJ[:, a.r, 0:N], ACT.Square, accum_out=degree[:, a.r:a.r + 1])\
                    .then_inc(degree_ready, 1)

            def exp_for_elu(a):
                act.wait_ge(sum_ready, a.t + 1)
                if a.after(1):
                    act.wait_ge(y_steps, 4 * (a.t - 1) + 2)
                act.activation(e_elu[:], acc_ps[a.s][:], ACT.Exp).then_inc(elu_exp_ready, 1)

            def exp_and_diag(a):
                act.wait_ge(softmax_steps, 4 * a.t + 4)
                if a.after(1):
                    act.wait_ge(weight_steps, 3 * a.t)
                act.activation(expd[:], logits[:], ACT.Exp, bias=neg_max[:], accum_out=den[:])\
                    .then_inc(exp_ready, 1)
                act.wait_ge(weight_steps, 3 * a.t + 3)
                if a.after(1):
                    act.wait_ge(sum_ready, a.t)
                for k in range(K + 1):
                    done = act.activation(diag[:, k, :], ident[:], ACT.Copy, scale=weight[:, k:k + 1])
                done.then_inc(diag_ready, 1)

            def step(a):
                if not (known(a.i) and a.c >= T):
                    count(a)
                if a.after(2):
                    exp_for_elu(a.back(2))
                if a.after(1) and not (known(a.i) and a.c > T):
                    exp_and_diag(a.back(1))

            over_tiles(act, step, 2 * RING, 2)


            def exps(g):
                act.wait_ge(dense_max, 4 * g + 4)
                for c in range(CH):
                    cols = slice(c * CW, (c + 1) * CW)
                    act.wait_ge(logits_ready, CH * g + c + 1)
                    act.activation(probs[:, cols], logit[:, cols], ACT.Exp, bias=neg_max[:],
                                   accum_out=chunk_den[:, c:c + 1]).then_inc(probs_ready, 1)

            def dense_round(g, more):
                for n in range(NB):
                    act.wait_ge(probsT_ready, NB * g + n + 1)
                    if n >= 2:
                        act.wait_ge(dense_sum, NB * g + n - 1)
                    act.activation(probsT[n % 2], xT_ps[n % 2][:], ACT.Copy).then_inc(probsT_copied, 1)
                act.wait_ge(dense_steps, 7 * g + 3)
                act.activation(rows_e, rows_sum, ACT.Exp).then_inc(dense_exp, 1)
                with more():
                    exps(g + 1)

            rounds(act, lambda: exps(0), dense_round)

        @block.gpsimd
        def _(pool):
            pool.memset(ones[:], 1.0).then_inc(consts_ready, 1)
            pool.memset(minus_half[:], -0.5).then_inc(consts_ready, 1)
            pool.memset(eps[:], EPS).then_inc(consts_ready, 1)
            pool.memset(zero2[:], 0.0).then_inc(consts_ready, 1)
            pool.wait_ge(consts_ready, 4)
            pool.affine_select(out=ident[:], in_=ones[:], pattern=[[-1, P]], compare_op=ALU.is_equal,
                               fill=0.0, base=0, channel_multiplier=1).then_inc(consts_ready, 1)
            pool.memset(h_sum, 0.0).then_inc(h_used, 1)

            def use_h(g, b):
                pool.wait_ge(h_copied, g + 1)
                pool.wait_ge(h_used, g + 1)
                pool.tensor_tensor(S12[:, bass.ds(GROUP * g, GROUP), :], HB[b][:, :, D:DA], zero2[:], ALU.add)
                pool.tensor_tensor(h_sum, h_sum, HB[b], ALU.add).then_inc(h_used, 1)

            use_h(0, 0)
            use_h(1, 1)
            with pool.Fori(1, G // 2) as i:
                for b in range(2):
                    use_h(2 * i + b, b)
            pool.wait_ge(h_used, G + 1)
            pool.tensor_tensor(h_sum[:, 0, :], h_sum[:, 0, :], h_sum[:, 1, :], ALU.add).then_inc(h_summed, 1)
            for b in range(2):
                pool.wait_ge(h_stored[b], 16 * (G // 2))
            pool.wait_ge(h_mean_ps, 1)
            pool.memset(gath_flat, 0.0).then_inc(gath_zeroed, 1)
            pool.wait_ge(gath_zeroed, 1)
            pool.affine_select(out=before, in_=ones[:], pattern=[[1, P]], compare_op=ALU.is_gt, fill=0.0,
                               base=0, channel_multiplier=-1).then_inc(dense_consts, 1)
            pool.iota(iota_q, pattern=[[1, P]], base=0, channel_multiplier=0,
                      allow_small_or_imprecise_dtypes=True).then_inc(dense_consts, 1)
            pool.iota(row_ids[:, :, 0], pattern=[[1, T]], base=0, channel_multiplier=0,
                      allow_small_or_imprecise_dtypes=True).then_inc(dense_consts, 1)
            pool.iota(row_ids[:, :, 1], pattern=[[0, T]], base=0, channel_multiplier=1,
                      allow_small_or_imprecise_dtypes=True).then_inc(dense_consts, 1)
            pool.memset(row_ids[:, :, 2], 1.0).then_inc(dense_consts, 1)

            def gather(a):
                pool.wait_ge(columns_found, a.t + 1)
                if a.after(RING):
                    pool.wait_ge(sum_ready, a.t - RING + 1)
                if a.after(1):
                    pool.wait_ge(gate_passed, a.t)
                pool.tensor_tensor(pool_gate[:], minus_half[:], minus_half[:], ALU.add)\
                    .then_inc(gate_passed, 1)
                for k in range(K):
                    pool.indirect_dma_start(
                        out=GATH[:, a.r, k * DA:(k + 1) * DA], out_offset=None, in_=haug,
                        in_offset=bass.IndirectOffsetOnAxis(ap=found_at[:, a.r, k:k + 1], axis=0),
                        bounds_check=N - 1, oob_is_err=False).then_inc(gathered[a.r], 16)

            def normalise(a):
                pool.wait_ge(y_steps, 4 * a.t + 4)
                if a.after(1):
                    pool.wait_ge(row_normed, a.t)
                pool.tensor_tensor(veps[:], mean_var[:, a.r, 1:2], eps[:], ALU.add).then_inc(norm_steps, 1)
                pool.wait_ge(norm_steps, 3 * a.t + 1)
                pool.tensor_tensor(rstd[:], veps[:], minus_half[:], ALU.pow).then_inc(norm_steps, 1)
                pool.tensor_tensor(Y[:, a.r, :], Y[:, a.r, :], mean_var[:, a.r, 0:1].broadcast_to([P, D]),
                                   ALU.subtract).then_inc(norm_steps, 1)
                pool.wait_ge(norm_steps, 3 * a.t + 3)
                pool.tensor_tensor(Y[:, a.r, :], Y[:, a.r, :], rstd[:].broadcast_to([P, D]), ALU.mult)\
                    .then_inc(row_normed, 1)

            def step(a):
                if not (known(a.i) and a.c >= T):
                    gather(a)
                if a.after(3):
                    normalise(a.back(3))

            over_tiles(pool, step, RING, 3)

            for r in range(RING):
                pool.wait_ge(out_stored[r], 16 * len(range(r, T, RING)))

            pool.tensor_tensor(veps[:], minus_half[:], minus_half[:], ALU.add).then_inc(round_open, 1)

            def prepare(g):
                rows = bass.IndirectOffsetOnAxis(ap=next_rows[:], axis=0)
                if not known(g) or g >= 1:
                    pool.wait_ge(probs_ready, CH * g)
                pool.wait_ge(list_steps, (4 + CH) * g + 4 + CH)
                at = 0 if known(g) else 1
                pool.tensor_tensor(pool_gates[:, at:at + 1], minus_half[:], minus_half[:], ALU.add)
                for c in range(CH):
                    pool.indirect_dma_start(
                        out=rows_adj[:, c * CW:(c + 1) * CW], out_offset=None,
                        in_=adj.rearrange("n (c w) -> (n c) w", c=CH),
                        in_offset=bass.IndirectOffsetOnAxis(ap=next_parts[:, c:c + 1], axis=0),
                        bounds_check=N * CH - 1, oob_is_err=False).then_inc(adj_gathered[c], 16)
                    if c == 0:
                        pool.indirect_dma_start(out=rows_h, out_offset=None, in_=haug, in_offset=rows,
                                                bounds_check=N - 1, oob_is_err=False).then_inc(rows_gathered, 16)

            def dense_round(g, more):
                rows = bass.IndirectOffsetOnAxis(ap=round_rows[:], axis=0)
                pool.wait_ge(list_steps, (4 + CH) * (g + 1))
                pool.tensor_tensor(pool_gates[:, 2:3], minus_half[:], minus_half[:], ALU.add)
                pool.tensor_copy(round_rows[:], next_rows[:]).then_inc(round_taken, 1)
                pool.wait_ge(round_taken, g + 1)
                pool.tensor_tensor(pool_gates[:, 4:5], minus_half[:], minus_half[:], ALU.add)
                pool.indirect_dma_start(out=rows_x, out_offset=None, in_=x, in_offset=rows,
                                        bounds_check=N - 1, oob_is_err=False).then_inc(x_gathered, 16)
                with more():
                    prepare(g + 1)
                pool.wait_ge(dense_steps, 7 * g + 7)
                pool.tensor_tensor(veps[:], mean_var[:, 0, 1:2], eps[:], ALU.add).then_inc(dense_norm, 1)
                pool.wait_ge(dense_norm, 4 * g + 1)
                pool.tensor_tensor(rstd[:], veps[:], minus_half[:], ALU.pow).then_inc(dense_norm, 1)
                pool.tensor_tensor(rows_y, rows_y, mean_var[:, 0, 0:1].broadcast_to([P, D]), ALU.subtract)\
                    .then_inc(dense_norm, 1)
                pool.wait_ge(dense_norm, 4 * g + 3)
                pool.tensor_tensor(rows_y, rows_y, rstd[:].broadcast_to([P, D]), ALU.mult).then_inc(dense_norm, 1)
                pool.wait_ge(dense_norm, 4 * g + 4)
                pool.tensor_tensor(pool_gates[:, 3:4], minus_half[:], minus_half[:], ALU.add)
                pool.indirect_dma_start(out=out, out_offset=rows, in_=rows_y, in_offset=None,
                                        bounds_check=N - 1, oob_is_err=False).then_inc(rows_stored, 16)
                pool.wait_ge(rows_stored, 16 * g + 16)
                pool.tensor_tensor(veps[:], minus_half[:], minus_half[:], ALU.add).then_inc(round_open, 1)

            rounds(pool, lambda: prepare(0), dense_round)


_INS = ['x', 'adj', 'L0_gnn_W', 'L0_gnn_attn']


def kernel(**inputs):
    import concourse.bacc as _bacc
    from concourse import mybir as _mybir
    from concourse.bass_utils import run_bass_kernel_spmd as _run

    nc = _bacc.Bacc("TRN2", target_bir_lowering=False, num_devices=1)
    arrays, args = {}, []
    for name in _INS:
        a = np.ascontiguousarray(inputs[name])
        arrays[f"in_{name}_dram"] = a
        args.append(nc.dram_tensor(f"in_{name}_dram", a.shape, _mybir.dt.from_np(a.dtype),
                                   kind="ExternalInput").ap())
    shape = inputs['x'].shape
    args.append(nc.dram_tensor("out_0_dram", shape, _mybir.dt.float32, kind="ExternalOutput").ap())
    gat_resnorm(nc, *args)
    r = _run(nc, [arrays], core_ids=[0])
    return r.results[0]["out_0_dram"]
```

```python
from contextlib import ExitStack

import numpy as np

import concourse.bass as bass
from concourse import mybir

F32 = mybir.dt.float32
I32 = mybir.dt.int32
U32 = mybir.dt.uint32
U8 = mybir.dt.uint8
BF16 = mybir.dt.bfloat16
ALU = mybir.AluOpType
ACT = mybir.ActivationFunctionType
AX_X = mybir.AxisListType.X

P = 128
SLOPE = 0.2
NEG_BIG = -9.0e15
EPS = 1e-5
FOUND = 8
K = 7
MAY_SKIP = 3
DIGIT = 256
FEW = 2
RING = 3


def gat_resnorm(nc, x, adj, W, attn, out):
    N, D = x.shape
    T = N // P
    C = D // P
    DA = D + 2
    GROUP = 2
    G = T // GROUP

    x_tiles = x.rearrange("(t p) d -> p t d", p=P)
    adj_tiles = adj.rearrange("(t p) n -> p t n", p=P)
    out_tiles = out.rearrange("(t p) d -> p t d", p=P)
    haug = nc.dram_tensor("haug", (N, DA), F32).ap()
    s2_row = nc.dram_tensor("s2_row", (T, P), F32).ap()
    haug_groups = haug.rearrange("(g u p) d -> p g u d", p=P, u=GROUP)

    with ExitStack() as ctx:
        def sb(name, shape, dt):
            return ctx.enter_context(nc.sbuf_tensor(name, shape, dt))

        def ps(name, shape):
            return ctx.enter_context(nc.psum_tensor(name, shape, F32))

        def sem(name):
            return ctx.enter_context(nc.semaphore(name))

        X = sb("X", [P, T, D], F32)
        ADJ = sb("ADJ", [P, RING, N + FOUND], I32)
        GATH = sb("GATH", [P, RING, K * DA], F32)
        count_junk = sb("count_junk", [P, N], U8)
        ident = sb("ident", [P, P], F32)
        ones = sb("ones", [P, P], F32)
        Waug = sb("Waug", [P, C, DA], F32)
        mean_h = sb("mean_h", [P, D], F32)
        diag = sb("diag", [P, K + 1, P], F32)
        S12 = sb("S12", [P, T, 2], F32)
        heavy = sb("heavy", [P, T], F32)
        found_at = sb("found_at", [P, RING, FOUND], U32)
        one8 = sb("one8", [P, FOUND], F32)
        gate = sb("gate", [P, 2, RING], F32)
        pool_gate = sb("pool_gate", [P, 2], F32)
        pool_gates = sb("pool_gates", [P, 5], F32)
        slot_digit = sb("slot_digit", [P, MAY_SKIP], F32)
        slots_used = sb("slots_used", [1, RING], I32)
        zero2 = sb("zero2", [P, GROUP, 2], F32)
        degree = sb("degree", [P, RING], F32)
        valid = sb("valid", [P, RING, K], F32)
        found = sb("found", [P, RING], F32)
        penalty = sb("penalty", [P, RING, K], F32)
        z = sb("z", [P, K], F32)
        lz = sb("lz", [P, K], F32)
        logits = sb("logits", [P, K], F32)
        row_max = sb("row_max", [P, 1], F32)
        neg_max = sb("neg_max", [P, 1], F32)
        expd = sb("expd", [P, K], F32)
        den = sb("den", [P, 1], F32)
        rden = sb("rden", [P, 1], F32)
        weight = sb("weight", [P, K + 1], F32)
        e_elu = sb("e_elu", [P, D], F32)
        stats = sb("stats", [P, 6], F32)
        mean_var = sb("mean_var", [P, RING, 2], F32)
        veps = sb("veps", [P, 1], F32)
        rstd = sb("rstd", [P, 1], F32)
        Y = sb("Y", [P, RING, D], F32)
        eps = sb("eps", [P, 1], F32)
        minus_half = sb("minus_half", [P, 1], F32)

        gath_flat = GATH[:].rearrange("p r f -> p (r f)")
        taken = [0]

        def in_gath(n):
            at = taken[0]
            taken[0] += n
            return gath_flat[:, at:at + n]

        HB = [in_gath(GROUP * DA).rearrange("p (u d) -> p u d", u=GROUP) for _ in range(2)]
        XS = [in_gath(GROUP * D).rearrange("p (u d) -> p u d", u=GROUP) for _ in range(2)]
        XT = [in_gath(GROUP * D) for _ in range(2)]
        h_sum = in_gath(GROUP * DA).rearrange("p (u d) -> p u d", u=GROUP)
        W_T_flat = in_gath(C * D)
        W_T = W_T_flat.rearrange("p (o k) -> p o k", o=C)
        a12_flat = in_gath(2 * C)
        a12 = a12_flat.rearrange("p (a o) -> p o a", o=C)

        CH = 4
        CW = N // CH
        rows_adj = ADJ[:, 0, 0:N]
        logit = ADJ[:, 0, 0:N].bitcast(F32)
        s2_all = ADJ[:, 1, 0:N].bitcast(F32)
        probs = ADJ[:, 2, 0:N].bitcast(F32)
        H = X
        behind = gath_flat[:, K * DA:]
        rows_h = behind[:, 0:DA]
        rows_x = behind[:, 260:260 + D]
        rows_y = behind[:, 516:516 + D]
        rows_e = behind[:, 772:772 + D]
        rows_sum = behind[:, 1028:1028 + D]
        slope_z = behind[:, 1284:1284 + CW]
        probsT = [diag[:, 4 * b:4 * b + 4, :].rearrange("p a b -> p (a b)") for b in range(2)]
        TH = T // 2
        onehot = count_junk[:].bitcast(BF16).rearrange("p (t q) -> p t q", t=TH)
        before = Waug[:, 1, 0:P]
        iota_q = Waug[:, 1, P:2 * P]
        row_ids = sb("row_ids", [P, T, 3], BF16)
        heavyT = Waug[0:T, 0, 0:P]
        s2T = Waug[0:T, 0, P:2 * P]
        heavy_in_row = sb("heavy_in_row", [P, 1], F32)
        rank = sb("rank", [P, T], F32)
        n_heavy = sb("n_heavy", [P, 1], I32)
        listed = sb("listed", [P, 3], F32)
        list_id = sb("list_id", [P, 2], F32)
        next_rows = sb("next_rows", [P, 1], U32)
        next_parts = sb("next_parts", [P, CH], U32)
        round_rows = sb("round_rows", [P, 1], U32)
        dense_gate = sb("dense_gate", [P, 6], F32)
        chunk_max = sb("chunk_max", [P, CH], F32)
        chunk_den = sb("chunk_den", [P, CH], F32)

        xT_ps = [ps(f"xT_ps{b}", [P, GROUP * D]) for b in range(2)]
        h_ps = [ps(f"h_ps{b}", [P, GROUP, 512]) for b in range(2)]
        acc_ps = [ps(f"acc_ps{b}", [P, D]) for b in range(2)]

        x_first_loaded = sem("x_first_loaded")
        x_loaded = [sem(f"x_loaded{i}") for i in range(4)]
        params_loaded = sem("params_loaded")
        adj_loaded = [sem(f"adj_loaded{r}") for r in range(RING)]
        consts_ready = sem("consts_ready")
        sentinels_ready = sem("sentinels_ready")
        wT_ready = sem("wT_ready")
        wT_copied = sem("wT_copied")
        wa_ready = sem("wa_ready")
        waug_ready = sem("waug_ready")
        x_staged = sem("x_staged")
        xT_ready = sem("xT_ready")
        xT_copied = sem("xT_copied")
        h_ready = sem("h_ready")
        h_copied = sem("h_copied")
        h_used = sem("h_used")
        h_stored = [sem(f"h_stored{b}") for b in range(2)]
        h_summed = sem("h_summed")
        h_mean_ps = sem("h_mean_ps")
        h_mean_ready = sem("h_mean_ready")
        gath_zeroed = sem("gath_zeroed")
        columns_found = sem("columns_found")
        degree_ready = sem("degree_ready")
        masks_ready = sem("masks_ready")
        slots_counted = sem("slots_counted")
        slots_noted = sem("slots_noted")
        gathered = [sem(f"gathered{r}") for r in range(RING)]
        softmax_steps = sem("softmax_steps")
        exp_ready = sem("exp_ready")
        weight_steps = sem("weight_steps")
        heavy_noted = sem("heavy_noted")
        diag_ready = sem("diag_ready")
        gate_passed = sem("gate_passed")
        sum_ready = sem("sum_ready")
        elu_exp_ready = sem("elu_exp_ready")
        y_steps = sem("y_steps")
        norm_steps = sem("norm_steps")
        row_normed = sem("row_normed")
        out_stored = [sem(f"out_stored{r}") for r in range(RING)]

        XL = T // 4
        XF = 2 * GROUP
        QC = G // 8
        adj_chunks = [2 * QC, QC, QC]
        x_loads = [1, 1, QC, QC]

        dense_consts = sem("dense_consts")
        h_loaded = sem("h_loaded")
        h_last_loaded = sem("h_last_loaded")
        s2_stored = sem("s2_stored")
        s2_loaded = sem("s2_loaded")
        s2_turned = sem("s2_turned")
        s2_copied = sem("s2_copied")
        turned = sem("turned")
        turned_copied = sem("turned_copied")
        ranks_ready = sem("ranks_ready")
        rank_steps = sem("rank_steps")
        rank_ready = sem("rank_ready")
        onehot_ready = sem("onehot_ready")
        onehot_used = sem("onehot_used")
        list_steps = sem("list_steps")
        rows_gathered = sem("rows_gathered")
        x_gathered = sem("x_gathered")
        adj_gathered = [sem(f"adj_gathered{c}") for c in range(CH)]
        round_taken = sem("round_taken")
        slope_ready = sem("slope_ready")
        pen_ready = sem("pen_ready")
        masked_ready = sem("masked_ready")
        dense_max = sem("dense_max")
        logits_ready = sem("logits_ready")
        probs_ready = sem("probs_ready")
        probsT_ready = sem("probsT_ready")
        probsT_copied = sem("probsT_copied")
        dense_sum = sem("dense_sum")
        dense_steps = sem("dense_steps")
        sum_taken = sem("sum_taken")
        dense_exp = sem("dense_exp")
        dense_norm = sem("dense_norm")
        rows_stored = sem("rows_stored")
        round_open = sem("round_open")

        HL = 8
        TB = 4
        NB = T // TB

        def heavy_rows(eng):
            eng.wait_ge(rank_steps, 2)
            return eng.value_load(n_heavy[0:1, 0:1], min_val=0, max_val=N)

        def rounds(eng, n, first, body):
            def skipping(start, count):
                each = count // 4
                with eng.Fori(0, 4) as i:
                    g = start + i * each
                    with eng.If(n > g * P):
                        if each > 1:
                            skipping(g, each)
                        else:
                            body(g, lambda: eng.If(n > g * P + P))

            with eng.If(n > 0):
                if first:
                    first()
                skipping(0, T)

        block = ctx.enter_context(nc.Block())

        def known(g):
            return isinstance(g, int)

        class Tile:

            def __init__(self, i, c, unroll):
                self.i, self.c, self.unroll = i, c, unroll
                self.t = unroll * i + c
                self.r = c % RING
                self.s = c % 2
                self.loads = unroll // RING * i + c // RING + 1

            def back(self, n):
                return Tile(self.i, self.c - n, self.unroll)

            def after(self, n):
                assert known(self.i) or self.c >= n
                return self.c >= n

        FIRST, LAST = 6, 4

        def over_tiles(eng, step, unroll, upto=T):
            assert (T - FIRST - LAST) % unroll == 0
            for t in range(FIRST):
                step(Tile(0, t, unroll))
            with eng.Fori(0, (T - FIRST - LAST) // unroll) as i:
                for u in range(unroll):
                    step(Tile(i, FIRST + u, unroll))
            for t in range(T - LAST, upto):
                step(Tile(0, t, unroll))

        @block.sync
        def _(sp):
            sp.dma_start(Waug[:, :, 0:D], W.rearrange("(c p) d -> p c d", p=P)).then_inc(params_loaded, 16)
            sp.dma_start(a12_flat, attn.rearrange("(c p) one -> p (c one)", p=P),
                         allow_slow_non_contiguous=True).then_inc(params_loaded, 16)
            sp.dma_start(X[:, 0:XF, :], x_tiles[:, 0:XF, :]).then_inc(x_first_loaded, 16)
            sp.dma_start(X[:, XF:XL, :], x_tiles[:, XF:XL, :]).then_inc(x_loaded[0], 16)
            sp.dma_start(X[:, XL:2 * XL, :], x_tiles[:, XL:2 * XL, :]).then_inc(x_loaded[1], 16)

            def load_adj_chunk(tile, chunk):
                width = N // adj_chunks[tile]
                sp.dma_start(ADJ[:, tile, bass.ds(chunk * width, width)],
                             adj_tiles[:, tile, bass.ds(chunk * width, width)]).then_inc(adj_loaded[tile], 16)

            for q in range(4):
                with sp.Fori(0, QC) as c:
                    for b in range(2):
                        g = 2 * c + (2 * QC * q + b)
                        sp.wait_ge(h_copied, g + 1)
                        sp.dma_start(haug_groups[:, bass.ds(g, 1)], HB[b].unsqueeze(1)).then_inc(h_stored[b], 16)
                        if q < 2 and b == 0:
                            at = c * (XL // QC) + (q + 2) * XL
                            sp.dma_start(X[:, bass.ds(at, XL // QC), :], x_tiles[:, bass.ds(at, XL // QC), :])\
                                .then_inc(x_loaded[q + 2], 16)
                    if q < 2:
                        load_adj_chunk(0, c + q * QC)
                    else:
                        load_adj_chunk(q - 1, c)
            sp.wait_ge(s2_copied, 1)
            sp.dma_start(s2_row, s2T).then_inc(s2_stored, 16)

            def load_next(a):
                sp.wait_ge(columns_found, a.t + 1)
                sp.wait_ge(degree_ready, a.t + 1)
                sp.dma_start(ADJ[:, a.r, 0:N], adj_tiles[:, bass.ds(a.t + RING, 1), :])\
                    .then_inc(adj_loaded[a.r], 16)

            def store(a):
                sp.wait_ge(row_normed, a.t + 1)
                sp.dma_start(out_tiles[:, bass.ds(a.t, 1), :], Y[:, a.r:a.r + 1, :])\
                    .then_inc(out_stored[a.r], 16)

            peel = 4
            for t in range(peel):
                load_next(Tile(0, t, RING))
                if t >= 3:
                    store(Tile(0, t - 3, RING))
            with sp.Fori(0, (T - RING - peel) // RING) as i:
                for u in range(RING):
                    a = Tile(i, peel + u, RING)
                    load_next(a)
                    store(a.back(3))
            h_tiles = haug.rearrange("(t p) d -> p t d", p=P)[:, :, 0:D]

            def load_h(n):
                sp.dma_start(H[:, n * HL:(n + 1) * HL, :], h_tiles[:, n * HL:(n + 1) * HL, :])\
                    .then_inc(h_last_loaded if n == T // HL - 1 else h_loaded, 16)

            sp.wait_ge(y_steps, 4 * (T - HL))
            for n in range(3):
                load_h(n)
            for n, t in enumerate(range(T - RING - 3, T)):
                if t == T - 5:
                    sp.wait_ge(columns_found, T - 2)
                    sp.wait_ge(degree_ready, T - 2)
                    sp.wait_ge(s2_stored, 16)
                    sp.dma_start(s2_all, s2_row.rearrange("t p -> (t p)").partition_broadcast(P))\
                        .then_inc(s2_loaded, 16)
                store(Tile(0, t, RING))
                if n + 3 < T // HL - 1:
                    load_h(n + 3)
                if t == T - 2:
                    sp.wait_ge(y_steps, 4 * T)
                    load_h(T // HL - 1)
            for r in range(RING):
                sp.wait_ge(out_stored[r], 16 * len(range(r, T, RING)))
            sp.wait_ge(h_loaded, 16 * (T // HL - 1))
            sp.wait_ge(h_last_loaded, 16)
            sp.wait_ge(s2_loaded, 16)

        @block.tensor
        def _(pe):
            pe.wait_ge(params_loaded, 32)
            pe.wait_ge(consts_ready, 5 + MAY_SKIP)
            for o in range(C):
                for k in range(C):
                    done = nc.tensor.transpose(xT_ps[0][:, (o * C + k) * P:(o * C + k + 1) * P],
                                               Waug[:, k, o * P:(o + 1) * P], ident[:])
            done.then_inc(wT_ready, 1)
            pe.wait_ge(wT_copied, 1)
            for k in range(C):
                for o in range(C):
                    done = nc.tensor.matmul(h_ps[0][:, 0, 2 * k:2 * k + 2], W_T[:, o, k * P:(k + 1) * P],
                                            a12[:, o, :], start=(o == 0), stop=(o == C - 1))
            done.then_inc(wa_ready, 1)
            pe.wait_ge(waug_ready, 2)

            def transposes(g, b):
                pe.wait_ge(x_staged, g + 1)
                for u in range(GROUP):
                    for c in range(C):
                        at = (u * C + c) * P
                        done = nc.tensor.transpose(xT_ps[b][:, at:at + P],
                                                   XS[b][:, u, c * P:(c + 1) * P], ident[:])
                done.then_inc(xT_ready, 1)

            def project(g, b):
                pe.wait_ge(xT_copied, g + 1)
                if not known(g) or g >= 2:
                    pe.wait_ge(h_copied, g - 1)
                for u in range(GROUP):
                    for c in range(C):
                        at = (u * C + c) * P
                        done = nc.tensor.matmul(h_ps[b][:, u, 0:DA], XT[b][:, at:at + P], Waug[:, c, :],
                                                start=(c == 0), stop=(c == C - 1))
                done.then_inc(h_ready, 1)

            transposes(0, 0)
            transposes(1, 1)
            for b in range(2):
                project(b, b)
                transposes(b + 2, b)
            with pe.Fori(1, G // 2 - 1) as i:
                for b in range(2):
                    project(2 * i + b, b)
                    transposes(2 * i + b + 2, b)
            project(G - 2, 0)
            project(G - 1, 1)

            pe.wait_ge(h_summed, 1)
            nc.tensor.transpose(xT_ps[0][0:T, 0:P], S12[:, :, 1], ident[:]).then_inc(s2_turned, 1)
            nc.tensor.matmul(acc_ps[0][:], ones[:], h_sum[:, 0, 0:D], start=True, stop=True)\
                .then_inc(h_mean_ps, 1)
            pe.wait_ge(h_mean_ready, 1)

            def count_slots(a):
                pe.wait_ge(masks_ready, 3 * a.t + 3)
                if a.after(1):
                    pe.wait_ge(slots_noted, a.t)
                for j in range(MAY_SKIP):
                    k = K - MAY_SKIP + j
                    done = nc.tensor.matmul(h_ps[1][0:1, 0, 0:1], slot_digit[:, j:j + 1], valid[:, a.r, k:k + 1],
                                            start=(j == 0), stop=(j == MAY_SKIP - 1))
                done.then_inc(slots_counted, 1)

            def weighted_sum(a):
                pe.wait_ge(diag_ready, a.t + 1)
                if a.after(2):
                    pe.wait_ge(y_steps, 4 * (a.t - 1))
                    pe.wait_ge(elu_exp_ready, a.t - 1)
                for k in range(K + 1):
                    rows = GATH[:, a.r, k * DA:k * DA + D] if k < K else mean_h[:]
                    done = nc.tensor.matmul(acc_ps[a.s][:], diag[:, k, :], rows, start=(k == 0), stop=(k == K))
                done.then_inc(sum_ready, 1)

            def list_rows(g, half):
                pe.wait_ge(onehot_ready, 2 * g + half + 1)
                for t in range(TH):
                    done = nc.tensor.matmul(h_ps[0][:, 0, 0:3], onehot[:, t, :], row_ids[:, half * TH + t, :],
                                            start=(half == 0 and t == 0), stop=(half == 1 and t == TH - 1))
                done.then_inc(onehot_used, 1)

            def step(a):
                count_slots(a)
                if a.after(1):
                    weighted_sum(a.back(1))

            over_tiles(pe, step, 2 * RING, upto=T - 3)
            tiles = [Tile(0, t, 2 * RING) for t in range(T)]
            count_slots(tiles[T - 3])
            count_slots(tiles[T - 2])
            weighted_sum(tiles[T - 4])
            count_slots(tiles[T - 1])


            pe.wait_ge(heavy_noted, T)
            pe.wait_ge(dense_consts, 5)
            nc.tensor.transpose(xT_ps[0][0:T, 0:P], heavy[:], ident[:]).then_inc(turned, 1)
            pe.wait_ge(turned_copied, 2)
            nc.tensor.matmul(xT_ps[1][:, 0:T], heavyT, before[0:T, 0:T], start=True, stop=False)
            nc.tensor.matmul(xT_ps[1][:, 0:T], before, heavy_in_row[:].broadcast_to([P, T]),
                             start=False, stop=True)
            nc.tensor.matmul(h_ps[0][:, 0, 0:1], ones[:], heavy_in_row[:], start=True, stop=True)\
                .then_inc(ranks_ready, 1)
            n = heavy_rows(pe)
            with pe.If(n > 0):
                list_rows(0, 0)
                list_rows(0, 1)
            for t in range(T - 3, T):
                weighted_sum(tiles[t])
            pe.wait_ge(h_loaded, 16 * (T // HL - 1))

            def dense_round(g, more):
                for n in range(NB + 1):
                    if n in (2, 4):
                        with more():
                            list_rows(g + 1, n // 2 - 1)
                    if n < NB:
                        if n % (NB // CH) == 0:
                            pe.wait_ge(probs_ready, CH * g + n // (NB // CH) + 1)
                        if n >= 2:
                            pe.wait_ge(probsT_copied, NB * g + n - 1)
                        for u in range(TB):
                            at = (n * TB + u) * P
                            done = nc.tensor.transpose(xT_ps[n % 2][:, u * P:(u + 1) * P], probs[:, at:at + P],
                                                       ident[:])
                        done.then_inc(probsT_ready, 1)
                    if n >= 1:
                        m = n - 1
                        pe.wait_ge(probsT_copied, NB * g + m + 1)
                        if m == 0:
                            pe.wait_ge(sum_taken, g + 1)
                        if m == NB - HL // TB:
                            pe.wait_ge(h_last_loaded, 16)
                        for u in range(TB):
                            done = nc.tensor.matmul(acc_ps[0][:], probsT[m % 2][:, u * P:(u + 1) * P],
                                                    H[:, m * TB + u, :], start=(m == 0 and u == 0),
                                                    stop=(m == NB - 1 and u == TB - 1))
                        done.then_inc(dense_sum, 1)

            rounds(pe, n, None, dense_round)

        @block.vector
        def _(dve):
            dve.memset(one8[:], 1.0).then_inc(sentinels_ready, 1)
            dve.memset(ADJ[:, :, N:N + FOUND], 1).then_inc(sentinels_ready, 1)
            dve.wait_ge(wT_ready, 1)
            dve.tensor_copy(W_T_flat, xT_ps[0][:, 0:C * C * P]).then_inc(wT_copied, 1)
            dve.wait_ge(wa_ready, 1)
            for k in range(C):
                dve.tensor_copy(Waug[:, k, D:DA], h_ps[0][:, 0, 2 * k:2 * k + 2]).then_inc(waug_ready, 1)

            def stage_x(g, b):
                dve.tensor_copy(XS[b], X[:, bass.ds(GROUP * g, GROUP), :]).then_inc(x_staged, 1)

            def copy_xT(g, b):
                dve.wait_ge(xT_ready, g + 1)
                if not known(g) or g >= 2:
                    dve.wait_ge(h_ready, g - 1)
                dve.tensor_copy(XT[b], xT_ps[b][:]).then_inc(xT_copied, 1)

            GL = XL // GROUP
            dve.wait_ge(x_first_loaded, 16)
            stage_x(0, 0)
            stage_x(1, 1)
            for g in range(2):
                copy_xT(g, g)
                dve.wait_ge(x_loaded[0], 16)
                stage_x(g + 2, g)
            for i in range(4):
                dve.wait_ge(x_loaded[i], 16 * x_loads[i])
                with dve.Fori(max(GL // 2 * i - 1, 1), GL // 2 * (i + 1) - 1) as j:
                    for b in range(2):
                        copy_xT(2 * j + b, b)
                        stage_x(2 * j + b + 2, b)
            copy_xT(G - 2, 0)
            copy_xT(G - 1, 1)

            def masks(a):
                dve.wait_ge(columns_found, a.t + 1)
                dve.tensor_scalar(valid[:, a.r, :], found_at[:, a.r, 0:K], float(N) - 0.5, None, ALU.is_lt)\
                    .then_inc(masks_ready, 1)
                dve.tensor_scalar(penalty[:, a.r, :], found_at[:, a.r, 0:K], float(N) - 0.5, NEG_BIG,
                                  ALU.is_gt, ALU.mult).then_inc(masks_ready, 1)
                dve.wait_ge(masks_ready, 3 * a.t + 2)
                dve.tensor_reduce(found[:, a.r:a.r + 1], valid[:, a.r, :], AX_X, ALU.add)\
                    .then_inc(masks_ready, 1)

            def note_heavy(a):
                dve.wait_ge(degree_ready, a.t + 1)
                dve.wait_ge(masks_ready, 3 * a.t + 3)
                dve.tensor_tensor(heavy[:, bass.ds(a.t, 1)], degree[:, a.r:a.r + 1], found[:, a.r:a.r + 1],
                                  ALU.not_equal).then_inc(heavy_noted, 1)

            def note_slots(a):
                dve.wait_ge(slots_counted, a.t + 1)
                dve.tensor_copy(slots_used[0:1, a.r:a.r + 1], h_ps[1][0:1, 0, 0:1]).then_inc(slots_noted, 1)

            def logits_and_residual(a, b, c):
                if a:
                    dve.wait_ge(gathered[a.r], 16 * K * a.loads)
                    dve.wait_ge(masks_ready, 3 * a.t + 3)
                    if a.after(1):
                        dve.wait_ge(exp_ready, a.t)
                    s2 = GATH[:, a.r, :].rearrange("p (k d) -> p k d", k=K)[:, :, D + 1]
                    dve.tensor_scalar(z[:], s2, S12[:, bass.ds(a.t, 1), 0], None, ALU.add)\
                        .then_inc(softmax_steps, 1)
                if b:
                    y = Y[:, b.r, :]
                    dve.wait_ge(sum_ready, b.t + 1)
                    dve.wait_ge(elu_exp_ready, b.t + 1)
                    if b.after(RING):
                        dve.wait_ge(out_stored[b.r], 16 * (b.loads - 1))
                    dve.scalar_tensor_tensor(out=Y[:, b.r:b.r + 1, :], in0=acc_ps[b.s][:].unsqueeze(1),
                                             scalar=0.0, in1=X[:, bass.ds(b.t, 1), :], op0=ALU.max,
                                             op1=ALU.add).then_inc(y_steps, 1)
                if c:
                    note_slots(c)
                if a:
                    dve.wait_ge(softmax_steps, 4 * a.t + 1)
                    dve.scalar_tensor_tensor(out=lz[:], in0=z[:], scalar=SLOPE, in1=z[:], op0=ALU.mult,
                                             op1=ALU.max).then_inc(softmax_steps, 1)
                if b:
                    dve.wait_ge(y_steps, 4 * b.t + 1)
                    dve.scalar_tensor_tensor(out=y, in0=e_elu[:], scalar=1.0, in1=y, op0=ALU.min,
                                             op1=ALU.add).then_inc(y_steps, 1)
                if a:
                    dve.wait_ge(softmax_steps, 4 * a.t + 2)
                    dve.tensor_tensor(logits[:], lz[:], penalty[:, a.r, :], ALU.add).then_inc(softmax_steps, 1)
                if b:
                    dve.wait_ge(y_steps, 4 * b.t + 2)
                    dve.bn_stats(stats[:], y).then_inc(y_steps, 1)
                if a:
                    dve.wait_ge(softmax_steps, 4 * a.t + 3)
                    dve.tensor_reduce(neg_max[:], logits[:], AX_X, ALU.max, negate=True)\
                        .then_inc(softmax_steps, 1)
                if b:
                    dve.wait_ge(y_steps, 4 * b.t + 3)
                    if b.after(RING):
                        dve.wait_ge(row_normed, b.t - RING + 1)
                    dve.memset(gate[:, 1, b.r:b.r + 1], 0.0)
                    dve.bn_aggr(mean_var[:, b.r, :], stats[:]).then_inc(y_steps, 1)

            def weights_of(a):
                dve.wait_ge(exp_ready, a.t + 1)
                if a.after(1):
                    dve.wait_ge(diag_ready, a.t)
                dve.reciprocal(rden[:], den[:]).then_inc(weight_steps, 1)
                dve.tensor_scalar(weight[:, K:K + 1], found[:, a.r:a.r + 1], 0.0, None, ALU.is_equal)\
                    .then_inc(weight_steps, 1)
                dve.wait_ge(weight_steps, 3 * a.t + 2)
                dve.scalar_tensor_tensor(out=weight[:, 0:K], in0=expd[:], scalar=rden[:, 0:1],
                                         in1=valid[:, a.r, :], op0=ALU.mult, op1=ALU.mult)\
                    .then_inc(weight_steps, 1)

            def find(a):
                if a.after(RING):
                    dve.wait_ge(weight_steps, 3 * (a.t - RING + 1))
                dve.wait_ge(adj_loaded[a.r], 16 * (a.loads + adj_chunks[a.r] - 1))
                dve.memset(gate[:, 0, a.r:a.r + 1], 0.0)
                dve.max_index(found_at[:, a.r, :], one8[:], ADJ[:, a.r, :]).then_inc(columns_found, 1)
                masks(a)

            def step(a):
                if a.after(1):
                    note_heavy(a.back(1))
                    find(a)
                logits_and_residual(a.back(1) if a.after(1) else None, a.back(2) if a.after(2) else None, a)
                if a.after(1):
                    weights_of(a.back(1))

            dve.wait_ge(sentinels_ready, 2)
            find(Tile(0, 0, 2 * RING))
            dve.wait_ge(s2_turned, 1)
            dve.tensor_copy(s2T, xT_ps[0][0:T, 0:P]).then_inc(s2_copied, 1)
            dve.wait_ge(h_mean_ps, 1)
            dve.tensor_scalar(mean_h[:], acc_ps[0][:], 1.0 / N, None, ALU.mult).then_inc(h_mean_ready, 1)
            over_tiles(dve, step, 2 * RING, upto=T - 3)
            tiles = [Tile(0, t, 2 * RING) for t in range(T)]
            last = tiles[T - 1]
            for t in range(T - 3, T):
                note_heavy(tiles[t - 1])
                find(tiles[t])
                note_slots(tiles[t])
                if t == T - 2:
                    logits_and_residual(tiles[T - 4], tiles[T - 5], None)
                    weights_of(tiles[T - 4])

            note_heavy(last)
            dve.wait_ge(turned, 1)
            dve.tensor_copy(heavyT, xT_ps[0][0:T, 0:P]).then_inc(turned_copied, 1)
            dve.wait_ge(heavy_noted, T)
            dve.tensor_reduce(heavy_in_row[:], heavy[:], AX_X, ALU.add).then_inc(turned_copied, 1)
            dve.wait_ge(ranks_ready, 1)
            dve.scalar_tensor_tensor(out=rank[:], in0=xT_ps[1][:, 0:T], scalar=1.0, in1=heavy[:], op0=ALU.add,
                                     op1=ALU.mult).then_inc(rank_steps, 1)
            dve.tensor_copy(n_heavy[:], h_ps[0][:, 0, 0:1]).then_inc(rank_steps, 1)
            dve.wait_ge(rank_steps, 1)
            dve.tensor_scalar(rank[:], rank[:], -1.0, None, ALU.add).then_inc(rank_ready, 1)
            L = 4 + CH

            def mark_ranks(g, half):
                if half == 0:
                    dve.wait_ge(rank_ready, g + 1)
                    if known(g):
                        dve.wait_ge(dense_consts, 5)
                else:
                    dve.wait_ge(onehot_used, 2 * g + 1)
                dve.tensor_tensor(onehot, rank[:, half * TH:(half + 1) * TH].unsqueeze(2).broadcast_to([P, TH, P]),
                                  iota_q.unsqueeze(1).broadcast_to([P, TH, P]), ALU.is_equal)\
                    .then_inc(onehot_ready, 1)

            def finish_list(g):
                dve.wait_ge(onehot_ready, 2 * g + 2)
                dve.tensor_scalar(rank[:], rank[:], -float(P), None, ALU.add).then_inc(rank_ready, 1)
                if not known(g):
                    dve.wait_ge(round_taken, g)
                dve.wait_ge(onehot_used, 2 * g + 2)
                dve.tensor_copy(listed[:], h_ps[0][:, 0, 0:3]).then_inc(list_steps, 1)
                dve.wait_ge(list_steps, L * g + 1)
                dve.scalar_tensor_tensor(out=list_id[:, 0:1], in0=listed[:, 0:1], scalar=float(P),
                                         in1=listed[:, 1:2], op0=ALU.mult, op1=ALU.add).then_inc(list_steps, 1)
                dve.wait_ge(list_steps, L * g + 2)
                dve.scalar_tensor_tensor(out=list_id[:, 1:2], in0=listed[:, 2:3], scalar=-float(N),
                                         in1=list_id[:, 0:1], op0=ALU.mult, op1=ALU.add).then_inc(list_steps, 1)
                dve.wait_ge(list_steps, L * g + 3)
                dve.tensor_scalar(next_rows[:], list_id[:, 1:2], float(N), None, ALU.add).then_inc(list_steps, 1)
                for c in range(CH):
                    dve.tensor_scalar(next_parts[:, c:c + 1], list_id[:, 1:2], float(CH), float(CH * N + c),
                                      ALU.mult, ALU.add).then_inc(list_steps, 1)

            def mask_columns(g, chunks):
                for c in chunks:
                    cols = slice(c * CW, (c + 1) * CW)
                    dve.wait_ge(adj_gathered[c], 16 * g + 16)
                    dve.tensor_scalar(logit[:, cols], rows_adj[:, cols], 0.0, NEG_BIG / SLOPE, ALU.is_le, ALU.mult)\
                        .then_inc(pen_ready, 1)
                    dve.wait_ge(pen_ready, CH * g + c + 1)
                    dve.memset(dense_gate[:, c:c + 1], 0.0)
                    dve.tensor_tensor_reduce(logit[:, cols], logit[:, cols], s2_all[:, cols], 1.0, -3.0e38,
                                             ALU.add, ALU.max, chunk_max[:, c:c + 1]).then_inc(masked_ready, 1)

            def row_maxima(g):
                dve.wait_ge(masked_ready, CH * g + CH)
                dve.wait_ge(rows_gathered, 16 * g + 16)
                dve.tensor_reduce(row_max[:], chunk_max[:], AX_X, ALU.max).then_inc(dense_max, 1)
                dve.wait_ge(dense_max, 4 * g + 1)
                dve.tensor_tensor(z[:, 0:1], row_max[:], rows_h[:, D:D + 1], ALU.add).then_inc(dense_max, 1)
                dve.wait_ge(dense_max, 4 * g + 2)
                dve.scalar_tensor_tensor(out=lz[:, 0:1], in0=z[:, 0:1], scalar=SLOPE, in1=z[:, 0:1],
                                         op0=ALU.mult, op1=ALU.max).then_inc(dense_max, 1)
                dve.wait_ge(dense_max, 4 * g + 3)
                dve.tensor_scalar(neg_max[:], lz[:, 0:1], -1.0, None, ALU.mult).then_inc(dense_max, 1)

            def make_logits(g, chunks):
                for c in chunks:
                    cols = slice(c * CW, (c + 1) * CW)
                    if c >= 1:
                        dve.wait_ge(logits_ready, CH * g + c)
                    dve.tensor_scalar(slope_z, logit[:, cols], rows_h[:, D:D + 1], SLOPE, ALU.add, ALU.mult)\
                        .then_inc(slope_ready, 1)
                    dve.wait_ge(slope_ready, CH * g + c + 1)
                    dve.scalar_tensor_tensor(out=logit[:, cols], in0=logit[:, cols], scalar=rows_h[:, D:D + 1],
                                             in1=slope_z, op0=ALU.add, op1=ALU.max).then_inc(logits_ready, 1)

            def dense_round(g, more):
                with more():
                    mark_ranks(g + 1, 0)
                make_logits(g, [2])
                with more():
                    mark_ranks(g + 1, 1)
                make_logits(g, [3])
                with more():
                    finish_list(g + 1)
                dve.wait_ge(probs_ready, CH * g + CH)
                dve.tensor_reduce(den[:], chunk_den[:], AX_X, ALU.add).then_inc(dense_steps, 1)
                with more():
                    mask_columns(g + 1, range(CH))
                    row_maxima(g + 1)
                    make_logits(g + 1, [0])
                dve.wait_ge(dense_steps, 7 * g + 1)
                dve.reciprocal(rden[:], den[:]).then_inc(dense_steps, 1)
                dve.wait_ge(dense_steps, 7 * g + 2)
                dve.wait_ge(dense_sum, NB * g + NB)
                dve.wait_ge(round_open, g + 1)
                dve.tensor_scalar(rows_sum, acc_ps[0][:], rden[:, 0:1], None, ALU.mult).then_inc(dense_steps, 1)
                dve.wait_ge(dense_steps, 7 * g + 3)
                dve.memset(dense_gate[:, CH + 1:CH + 2], 0.0).then_inc(sum_taken, 1)
                dve.wait_ge(x_gathered, 16 * g + 16)
                dve.scalar_tensor_tensor(out=rows_y, in0=rows_sum, scalar=0.0, in1=rows_x, op0=ALU.max,
                                         op1=ALU.add).then_inc(dense_steps, 1)
                with more():
                    make_logits(g + 1, [1])
                dve.wait_ge(dense_steps, 7 * g + 4)
                dve.wait_ge(dense_exp, g + 1)
                dve.scalar_tensor_tensor(out=rows_y, in0=rows_e, scalar=1.0, in1=rows_y, op0=ALU.min,
                                         op1=ALU.add).then_inc(dense_steps, 1)
                dve.wait_ge(dense_steps, 7 * g + 5)
                dve.bn_stats(stats[:], rows_y).then_inc(dense_steps, 1)
                dve.wait_ge(dense_steps, 7 * g + 6)
                dve.memset(dense_gate[:, CH:CH + 1], 0.0)
                dve.bn_aggr(mean_var[:, 0, :], stats[:]).then_inc(dense_steps, 1)

            n = heavy_rows(dve)
            with dve.If(n > 0):
                mark_ranks(0, 0)
                mark_ranks(0, 1)
                finish_list(0)
            logits_and_residual(tiles[T - 3], tiles[T - 4], None)
            weights_of(tiles[T - 3])
            logits_and_residual(tiles[T - 2], None, None)
            weights_of(tiles[T - 2])
            with dve.If(n > 0):
                dve.wait_ge(s2_loaded, 16)
                mask_columns(0, range(CH // 2))
            logits_and_residual(None, tiles[T - 3], None)
            logits_and_residual(last, None, None)
            weights_of(last)
            with dve.If(n > 0):
                mask_columns(0, range(CH // 2, CH))
            logits_and_residual(None, tiles[T - 2], None)
            with dve.If(n > 0):
                row_maxima(0)
                dve.wait_ge(sum_ready, T - 1)
                make_logits(0, [0])
            logits_and_residual(None, last, None)
            dve.memset(dense_gate[:, CH + 1:CH + 2], 0.0).then_inc(sum_taken, 1)
            rounds(dve, n, lambda: make_logits(0, [1]), dense_round)

        @block.scalar
        def _(act):
            def copy_h(g, b):
                act.wait_ge(h_ready, g + 1)
                if not known(g) or g >= 2:
                    act.wait_ge(h_used, g)
                act.activation(HB[b], h_ps[b][:, :, 0:DA], ACT.Copy).then_inc(h_copied, 1)

            copy_h(0, 0)
            copy_h(1, 1)
            with act.Fori(1, G // 2) as i:
                for b in range(2):
                    g = 2 * i + b
                    act.wait_ge(h_ready, g + 1)
                    act.wait_ge(h_used, g)
                    act.wait_ge(h_stored[b], 16 * i)
                    act.activation(HB[b], h_ps[b][:, :, 0:DA], ACT.Copy).then_inc(h_copied, 1)

            def count(a):
                act.wait_ge(adj_loaded[a.r], 16 * (a.loads + adj_chunks[a.r] - 1))
                if a.after(1):
                    act.wait_ge(degree_ready, a.t)
                if a.after(RING):
                    act.wait_ge(heavy_noted, a.t - RING + 1)
                act.activation(count_junk[:], ADJ[:, a.r, 0:N], ACT.Square, accum_out=degree[:, a.r:a.r + 1])\
                    .then_inc(degree_ready, 1)

            def exp_for_elu(a):
                act.wait_ge(sum_ready, a.t + 1)
                if a.after(1):
                    act.wait_ge(y_steps, 4 * (a.t - 1) + 2)
                act.activation(e_elu[:], acc_ps[a.s][:], ACT.Exp).then_inc(elu_exp_ready, 1)

            def exp_and_diag(a):
                act.wait_ge(softmax_steps, 4 * a.t + 4)
                if a.after(1):
                    act.wait_ge(weight_steps, 3 * a.t)
                act.activation(expd[:], logits[:], ACT.Exp, bias=neg_max[:], accum_out=den[:])\
                    .then_inc(exp_ready, 1)
                act.wait_ge(weight_steps, 3 * a.t + 3)
                if a.after(1):
                    act.wait_ge(sum_ready, a.t)
                for k in range(K + 1):
                    done = act.activation(diag[:, k, :], ident[:], ACT.Copy, scale=weight[:, k:k + 1])
                done.then_inc(diag_ready, 1)

            def step(a):
                count(a)
                if a.after(2):
                    exp_for_elu(a.back(2))
                if a.after(1):
                    exp_and_diag(a.back(1))

            over_tiles(act, step, 2 * RING, upto=T - 3)
            tiles = [Tile(0, t, 2 * RING) for t in range(T)]
            count(tiles[T - 3])
            exp_for_elu(tiles[T - 5])
            count(tiles[T - 2])
            exp_and_diag(tiles[T - 4])
            count(tiles[T - 1])
            exp_for_elu(tiles[T - 4])
            exp_and_diag(tiles[T - 3])
            exp_and_diag(tiles[T - 2])
            exp_for_elu(tiles[T - 3])
            exp_and_diag(tiles[T - 1])
            exp_for_elu(tiles[T - 2])
            exp_for_elu(tiles[T - 1])

            def exps(g, c):
                cols = slice(c * CW, (c + 1) * CW)
                act.wait_ge(dense_max, 4 * g + 4)
                act.wait_ge(logits_ready, CH * g + c + 1)
                act.activation(probs[:, cols], logit[:, cols], ACT.Exp, bias=neg_max[:],
                               accum_out=chunk_den[:, c:c + 1]).then_inc(probs_ready, 1)

            exps_behind = (0, 3, 5)

            def dense_round(g, more):
                for n in range(NB):
                    act.wait_ge(probsT_ready, NB * g + n + 1)
                    if n >= 2:
                        act.wait_ge(dense_sum, NB * g + n - 1)
                    act.activation(probsT[n % 2], xT_ps[n % 2][:], ACT.Copy).then_inc(probsT_copied, 1)
                    if n in exps_behind:
                        exps(g, exps_behind.index(n) + 1)
                with more():
                    act.wait_ge(dense_steps, 7 * g + 1)
                    exps(g + 1, 0)
                act.wait_ge(dense_steps, 7 * g + 3)
                act.activation(rows_e, rows_sum, ACT.Exp).then_inc(dense_exp, 1)

            rounds(act, heavy_rows(act), lambda: exps(0, 0), dense_round)

        @block.gpsimd
        def _(pool):
            pool.memset(ones[:], 1.0).then_inc(consts_ready, 1)
            pool.memset(minus_half[:], -0.5).then_inc(consts_ready, 1)
            pool.memset(eps[:], EPS).then_inc(consts_ready, 1)
            pool.memset(zero2[:], 0.0).then_inc(consts_ready, 1)
            for j in range(MAY_SKIP):
                pool.memset(slot_digit[:, j:j + 1], float(DIGIT ** j)).then_inc(consts_ready, 1)
            pool.wait_ge(consts_ready, 4 + MAY_SKIP)
            pool.affine_select(out=ident[:], in_=ones[:], pattern=[[-1, P]], compare_op=ALU.is_equal,
                               fill=0.0, base=0, channel_multiplier=1).then_inc(consts_ready, 1)
            pool.memset(h_sum, 0.0).then_inc(h_used, 1)

            def use_h(g, b):
                pool.wait_ge(h_copied, g + 1)
                pool.wait_ge(h_used, g + 1)
                pool.tensor_tensor(S12[:, bass.ds(GROUP * g, GROUP), :], HB[b][:, :, D:DA], zero2[:], ALU.add)
                pool.tensor_tensor(h_sum, h_sum, HB[b], ALU.add).then_inc(h_used, 1)

            use_h(0, 0)
            use_h(1, 1)
            with pool.Fori(1, G // 2) as i:
                for b in range(2):
                    use_h(2 * i + b, b)
            pool.wait_ge(h_used, G + 1)
            pool.tensor_tensor(h_sum[:, 0, :], h_sum[:, 0, :], h_sum[:, 1, :], ALU.add).then_inc(h_summed, 1)
            for b in range(2):
                pool.wait_ge(h_stored[b], 16 * (G // 2))
            pool.wait_ge(h_mean_ps, 1)

            def dense_constants():
                pool.affine_select(out=before, in_=ones[:], pattern=[[1, P]], compare_op=ALU.is_gt, fill=0.0,
                                   base=0, channel_multiplier=-1).then_inc(dense_consts, 1)
                pool.iota(iota_q, pattern=[[1, P]], base=0, channel_multiplier=0,
                          allow_small_or_imprecise_dtypes=True).then_inc(dense_consts, 1)
                pool.iota(row_ids[:, :, 0], pattern=[[1, T]], base=0, channel_multiplier=0,
                          allow_small_or_imprecise_dtypes=True).then_inc(dense_consts, 1)
                pool.iota(row_ids[:, :, 1], pattern=[[0, T]], base=0, channel_multiplier=1,
                          allow_small_or_imprecise_dtypes=True).then_inc(dense_consts, 1)
                pool.memset(row_ids[:, :, 2], 1.0).then_inc(dense_consts, 1)

            def gather(a):
                if known(a.i) and a.c < RING:
                    pool.memset(GATH[:, a.r, :], 0.0).then_inc(gath_zeroed, 1)
                    pool.wait_ge(gath_zeroed, a.c + 1)
                pool.wait_ge(columns_found, a.t + 1)
                if a.after(RING):
                    pool.wait_ge(sum_ready, a.t - RING + 1)
                if a.after(1):
                    pool.wait_ge(gate_passed, 2 * a.t)
                pool.tensor_tensor(pool_gate[:, 0:1], minus_half[:], minus_half[:], ALU.add)\
                    .then_inc(gate_passed, 1)

                def slot(k, parts=P):
                    pool.indirect_dma_start(
                        out=GATH[0:parts, a.r, k * DA:(k + 1) * DA], out_offset=None, in_=haug,
                        in_offset=bass.IndirectOffsetOnAxis(ap=found_at[0:parts, a.r, k:k + 1], axis=0),
                        bounds_check=N - 1, oob_is_err=False).then_inc(gathered[a.r], 16)

                for k in range(K - MAY_SKIP):
                    slot(k)
                pool.wait_ge(slots_noted, a.t + 1)
                pool.tensor_tensor(pool_gate[:, 1:2], minus_half[:], minus_half[:], ALU.add)\
                    .then_inc(gate_passed, 1)
                used = pool.value_load(slots_used[0:1, a.r:a.r + 1], min_val=0,
                                       max_val=P * sum(DIGIT ** j for j in range(MAY_SKIP)))
                for j in range(MAY_SKIP):
                    with pool.If(used >= DIGIT ** j):
                        slot(K - MAY_SKIP + j)
                    with pool.If(used < DIGIT ** j):
                        slot(K - MAY_SKIP + j, FEW)

            def normalise(a):
                pool.wait_ge(y_steps, 4 * a.t + 4)
                if a.after(1):
                    pool.wait_ge(row_normed, a.t)
                pool.tensor_tensor(veps[:], mean_var[:, a.r, 1:2], eps[:], ALU.add).then_inc(norm_steps, 1)
                pool.wait_ge(norm_steps, 3 * a.t + 1)
                pool.tensor_tensor(rstd[:], veps[:], minus_half[:], ALU.pow).then_inc(norm_steps, 1)
                pool.tensor_tensor(Y[:, a.r, :], Y[:, a.r, :], mean_var[:, a.r, 0:1].broadcast_to([P, D]),
                                   ALU.subtract).then_inc(norm_steps, 1)
                pool.wait_ge(norm_steps, 3 * a.t + 3)
                pool.tensor_tensor(Y[:, a.r, :], Y[:, a.r, :], rstd[:].broadcast_to([P, D]), ALU.mult)\
                    .then_inc(row_normed, 1)

            def step(a):
                gather(a)
                if known(a.i) and a.c == RING:
                    dense_constants()
                if a.after(3):
                    normalise(a.back(3))

            over_tiles(pool, step, RING, upto=T - 1)
            gather(Tile(0, T - 1, RING))

            def prepare(g):
                rows = bass.IndirectOffsetOnAxis(ap=next_rows[:], axis=0)
                if not known(g) or g >= 1:
                    pool.wait_ge(probs_ready, CH * g)
                pool.wait_ge(list_steps, (4 + CH) * g + 4 + CH)
                at = 0 if known(g) else 1
                pool.tensor_tensor(pool_gates[:, at:at + 1], minus_half[:], minus_half[:], ALU.add)
                for c in range(CH):
                    pool.indirect_dma_start(
                        out=rows_adj[:, c * CW:(c + 1) * CW], out_offset=None,
                        in_=adj.rearrange("n (c w) -> (n c) w", c=CH),
                        in_offset=bass.IndirectOffsetOnAxis(ap=next_parts[:, c:c + 1], axis=0),
                        bounds_check=N * CH - 1, oob_is_err=False).then_inc(adj_gathered[c], 16)
                if known(g):
                    pool.wait_ge(sum_ready, T - 2)
                pool.indirect_dma_start(out=rows_h, out_offset=None, in_=haug, in_offset=rows,
                                        bounds_check=N - 1, oob_is_err=False).then_inc(rows_gathered, 16)

            def dense_round(g, more):
                rows = bass.IndirectOffsetOnAxis(ap=round_rows[:], axis=0)
                pool.wait_ge(list_steps, (4 + CH) * (g + 1))
                pool.tensor_tensor(pool_gates[:, 2:3], minus_half[:], minus_half[:], ALU.add)
                pool.tensor_copy(round_rows[:], next_rows[:]).then_inc(round_taken, 1)
                pool.wait_ge(round_taken, g + 1)
                pool.tensor_tensor(pool_gates[:, 4:5], minus_half[:], minus_half[:], ALU.add)
                pool.indirect_dma_start(out=rows_x, out_offset=None, in_=x, in_offset=rows,
                                        bounds_check=N - 1, oob_is_err=False).then_inc(x_gathered, 16)
                with more():
                    prepare(g + 1)
                pool.wait_ge(dense_steps, 7 * g + 7)
                pool.tensor_tensor(veps[:], mean_var[:, 0, 1:2], eps[:], ALU.add).then_inc(dense_norm, 1)
                pool.wait_ge(dense_norm, 4 * g + 1)
                pool.tensor_tensor(rstd[:], veps[:], minus_half[:], ALU.pow).then_inc(dense_norm, 1)
                pool.tensor_tensor(rows_y, rows_y, mean_var[:, 0, 0:1].broadcast_to([P, D]), ALU.subtract)\
                    .then_inc(dense_norm, 1)
                pool.wait_ge(dense_norm, 4 * g + 3)
                pool.tensor_tensor(rows_y, rows_y, rstd[:].broadcast_to([P, D]), ALU.mult).then_inc(dense_norm, 1)
                pool.wait_ge(dense_norm, 4 * g + 4)
                pool.tensor_tensor(pool_gates[:, 3:4], minus_half[:], minus_half[:], ALU.add)
                pool.indirect_dma_start(out=out, out_offset=rows, in_=rows_y, in_offset=None,
                                        bounds_check=N - 1, oob_is_err=False).then_inc(rows_stored, 16)
                pool.wait_ge(rows_stored, 16 * g + 16)
                pool.tensor_tensor(veps[:], minus_half[:], minus_half[:], ALU.add).then_inc(round_open, 1)

            n = heavy_rows(pool)
            with pool.If(n > 0):
                prepare(0)
            for t in range(T - 4, T):
                normalise(Tile(0, t, RING))
            for r in range(RING):
                pool.wait_ge(out_stored[r], 16 * len(range(r, T, RING)))
            pool.tensor_tensor(veps[:], minus_half[:], minus_half[:], ALU.add).then_inc(round_open, 1)
            rounds(pool, n, None, dense_round)


_INS = ['x', 'adj', 'L0_gnn_W', 'L0_gnn_attn']


def kernel(**inputs):
    import concourse.bacc as _bacc
    from concourse import mybir as _mybir
    from concourse.bass_utils import run_bass_kernel_spmd as _run

    nc = _bacc.Bacc("TRN2", target_bir_lowering=False, num_devices=1)
    arrays, args = {}, []
    for name in _INS:
        a = np.ascontiguousarray(inputs[name])
        arrays[f"in_{name}_dram"] = a
        args.append(nc.dram_tensor(f"in_{name}_dram", a.shape, _mybir.dt.from_np(a.dtype),
                                   kind="ExternalInput").ap())
    shape = inputs['x'].shape
    args.append(nc.dram_tensor("out_0_dram", shape, _mybir.dt.float32, kind="ExternalOutput").ap())
    gat_resnorm(nc, *args)
    r = _run(nc, [arrays], core_ids=[0])
    return r.results[0]["out_0_dram"]
```
